# Optimizing a Trainium2 kernel written in Bass

```python
import numpy as np
import jax
import jax.numpy as jnp

def _softmax(x, axis=-1):
    return jax.nn.softmax(x, axis=axis)

def _gelu(x):
    return jax.nn.gelu(x, approximate=True)

def _silu(x):
    return jax.nn.silu(x)

def _sigmoid(x):
    return jax.nn.sigmoid(x)

def _layernorm(x, axis=-1, eps=1e-05):
    m = jnp.mean(x, axis=axis, keepdims=True)
    v = jnp.var(x, axis=axis, keepdims=True)
    return (x - m) / jnp.sqrt(v + eps)

def _scatter_add(tgt, idx, src, axis=0):
    return tgt.at[idx].add(src)

def _segment_sum(src, seg, n):
    return jax.ops.segment_sum(src, seg, n)
kernel_name = 'mk_cond_resid_d4_seqx_r8_703cca'

def setup_inputs(seed: int=0):
    np.random.seed(seed)
    _w = jnp.asarray

    def _rec_inputs():
        import jax
        import jax.numpy as jnp
        _rk = jax.random.key(seed)
        x = -0.0003929 + 0.9999 * jax.random.normal(jax.random.fold_in(_rk, 1), (32, 128, 128), jnp.float32)
        _lenS = 128 - jax.random.randint(jax.random.fold_in(_rk, 7), (32,), 0, max(1, 128 // 4) + 1, jnp.int32)
        _lenS2 = 128 - jax.random.randint(jax.random.fold_in(_rk, 8), (32,), 0, max(1, 128 // 4) + 1, jnp.int32)
        itok_B_0_2 = jax.random.randint(jax.random.fold_in(_rk, 11), (32,), 0, 3, jnp.int32)
        itok_B_0_7 = jax.random.randint(jax.random.fold_in(_rk, 12), (32,), 0, 8, jnp.int32)
        fside_BxSxS_0 = 4.13588e-05 + 0.999923 * jax.random.normal(jax.random.fold_in(_rk, 13), (32, 128, 128), jnp.float32)
        itok_B_0_5 = jax.random.randint(jax.random.fold_in(_rk, 14), (32,), 0, 6, jnp.int32)
        return (x, itok_B_0_2, itok_B_0_7, fside_BxSxS_0, itok_B_0_5)
    x, itok_B_0_2, itok_B_0_7, fside_BxSxS_0, itok_B_0_5 = _rec_inputs()

    def _L0_cond_setup():
        import jax, jax.numpy as jnp
        import numpy as np
        NEG_INF = -1e+30
        key = jax.random.key(seed)
        k1, k2, k3, k4, k5 = jax.random.split(key, 5)
        B, S, D, A = (16, 128, 128, 32)
        hidden = jax.random.normal(k1, (B, S, D), dtype=jnp.float32)
        W1 = jax.random.normal(k2, (D, A), dtype=jnp.float32) / np.sqrt(D)
        b1 = jax.random.normal(k3, (A,), dtype=jnp.float32) * 0.01
        v = jax.random.normal(k4, (A,), dtype=jnp.float32) / np.sqrt(A)
        prompt_type_ids = jax.random.randint(k5, (B,), 0, 3, dtype=jnp.int32)
        return {'hidden': hidden, 'W1': W1, 'b1': b1, 'v': v, 'prompt_type_ids': prompt_type_ids}
    _L0_cond_all = _L0_cond_setup()
    _L0_cond_in = {k: v for k, v in _L0_cond_all.items() if k in ('W1', 'b1', 'v')}
    del _L0_cond_all

    def _L1_cond_setup():
        import jax, jax.numpy as jnp
        import numpy as np
        S, O, H = (8, 128, 128)
        B, N = (32, 64)
        key = jax.random.key(seed)
        k1, k2, k3, k4 = jax.random.split(key, 4)
        x = jax.random.normal(k1, (B, N, H), dtype=jnp.float32)
        subject_id = jax.random.randint(k2, (B,), 0, S)
        wbound = jnp.sqrt(2.0 / 6.0) * jnp.sqrt(3.0 / H)
        weight = jax.random.uniform(k3, (S, O, H), minval=-wbound, maxval=wbound, dtype=jnp.float32)
        bbound = 1.0 / jnp.sqrt(H)
        bias = jax.random.uniform(k4, (S, O), minval=-bbound, maxval=bbound, dtype=jnp.float32)
        return {'x': x, 'subject_id': subject_id, 'weight': weight, 'bias': bias}
    _L1_cond_all = _L1_cond_setup()
    _L1_cond_in = {k: v for k, v in _L1_cond_all.items() if k in ('weight', 'bias')}
    del _L1_cond_all

    def _L2_cond_setup():
        import jax, jax.numpy as jnp
        import numpy as np
        B, S, D, F, E = (8, 256, 128, 512, 5)

        def _dense(x, wi_, wo_):
            return jax.nn.relu(x @ wi_) @ wo_
        key = jax.random.key(seed)
        ks = jax.random.split(key, 9)
        sc = 0.02
        return {'hidden_states': jax.random.normal(ks[0], (B, S, D), jnp.float32), 'type_label': jax.random.randint(ks[1], (B,), 0, E, jnp.int32), 'wi': jax.random.normal(ks[2], (E, D, F), jnp.float32) * sc, 'wo': jax.random.normal(ks[3], (E, F, D), jnp.float32) * sc, 'swi': jax.random.normal(ks[4], (2, D, F), jnp.float32) * sc, 'swo': jax.random.normal(ks[5], (2, F, D), jnp.float32) * sc, 'g1': jax.random.normal(ks[6], (3 * D, D), jnp.float32) * sc, 'g2': jax.random.normal(ks[7], (D, 3), jnp.float32) * sc}
    _L2_cond_all = _L2_cond_setup()
    _L2_cond_in = {k: v for k, v in _L2_cond_all.items() if k in ('wi', 'wo', 'swi', 'swo', 'g1', 'g2')}
    del _L2_cond_all

    def _L3_cond_setup():
        import jax, jax.numpy as jnp
        import numpy as np
        B, S, D = (8, 128, 128)
        NUM_STAGES = 6
        key = jax.random.key(seed)
        k1, k2, k3, k4, k5 = jax.random.split(key, 5)
        return {'query': jax.random.normal(k1, (B, S, D), dtype=jnp.float32), 'key': jax.random.normal(k2, (B, S, D), dtype=jnp.float32), 'value': jax.random.normal(k3, (B, S, D), dtype=jnp.float32), 'braak_embed': jax.random.normal(k4, (NUM_STAGES, D), dtype=jnp.float32), 'braak_stages': jax.random.randint(k5, (B,), 0, NUM_STAGES, dtype=jnp.int64)}
    _L3_cond_all = _L3_cond_setup()
    _L3_cond_in = {k: v for k, v in _L3_cond_all.items() if k in ('braak_embed',)}
    del _L3_cond_all
    return {'x': x, 'itok_B_0_2': itok_B_0_2, 'itok_B_0_7': itok_B_0_7, 'fside_BxSxS_0': fside_BxSxS_0, 'itok_B_0_5': itok_B_0_5, 'L0_cond_W1': _L0_cond_in['W1'], 'L0_cond_b1': _L0_cond_in['b1'], 'L0_cond_v': _L0_cond_in['v'], 'L1_cond_weight': _L1_cond_in['weight'], 'L1_cond_bias': _L1_cond_in['bias'], 'L2_cond_wi': _L2_cond_in['wi'], 'L2_cond_wo': _L2_cond_in['wo'], 'L2_cond_swi': _L2_cond_in['swi'], 'L2_cond_swo': _L2_cond_in['swo'], 'L2_cond_g1': _L2_cond_in['g1'], 'L2_cond_g2': _L2_cond_in['g2'], 'L3_cond_braak_embed': _L3_cond_in['braak_embed']}

def reference(x, itok_B_0_2, itok_B_0_7, fside_BxSxS_0, itok_B_0_5, L0_cond_W1, L0_cond_b1, L0_cond_v, L1_cond_weight, L1_cond_bias, L2_cond_wi, L2_cond_wo, L2_cond_swi, L2_cond_swo, L2_cond_g1, L2_cond_g2, L3_cond_braak_embed):
    import jax
    import jax.numpy as jnp

    def _L0_cond_ref(hidden, W1, b1, v, prompt_type_ids):
        import jax, jax.numpy as jnp
        import numpy as np
        NEG_INF = -1e+30
        B, S, D = hidden.shape
        attn_in = jnp.tanh(jnp.einsum('bsd,da->bsa', hidden, W1) + b1)
        scores = jnp.einsum('bsa,a->bs', attn_in, v)
        idx = jnp.arange(S)
        j = idx[:, None]
        l = idx[None, :]
        prefix_m = l <= j
        postfix_m = l >= j
        cloze_m = l != j
        pt = prompt_type_ids[:, None, None]
        mask = jnp.where(pt == 0, prefix_m[None], jnp.where(pt == 1, postfix_m[None], cloze_m[None]))
        masked_scores = jnp.where(mask, scores[:, None, :], NEG_INF)
        p = jax.nn.softmax(masked_scores, axis=-1)
        cnt = jnp.sum(mask, axis=-1).astype(hidden.dtype)
        pooled = jnp.einsum('bjl,bld->bjd', p, hidden) / cnt[..., None]
        return pooled

    def _L1_cond_ref(x, subject_id, weight, bias):
        import jax, jax.numpy as jnp
        import numpy as np
        S, O, H = (8, 128, 128)
        B, N = (32, 64)
        W = weight[subject_id]
        b = bias[subject_id]
        y = jnp.einsum('bnh,boh->bno', x, W) + b[:, None, :]
        return y

    def _L2_cond_ref(hidden_states, type_label, wi, wo, swi, swo, g1, g2):
        import jax, jax.numpy as jnp
        import numpy as np
        B, S, D, F, E = (8, 256, 128, 512, 5)

        def _dense(x, wi_, wo_):
            return jax.nn.relu(x @ wi_) @ wo_
        x = hidden_states
        s0 = _dense(x, swi[0], swo[0])
        s1 = _dense(x, swi[1], swo[1])
        wi_sel = wi[type_label]
        wo_sel = wo[type_label]
        h = jax.nn.relu(jnp.einsum('bsd,bdf->bsf', x, wi_sel))
        eo = jnp.einsum('bsf,bfd->bsd', h, wo_sel)
        gate_in = jnp.concatenate([eo[:, 0], s0[:, 0], s1[:, 0]], axis=-1)
        w = jax.nn.softmax(jax.nn.relu(gate_in @ g1) @ g2, axis=-1)
        w = w[:, :, None, None]
        return eo * w[:, 0] + s0 * w[:, 1] + s1 * w[:, 2]

    def _L3_cond_ref(query, key, value, braak_embed, braak_stages):
        import jax, jax.numpy as jnp
        import numpy as np
        B, S, D = (8, 128, 128)
        NUM_STAGES = 6
        bias = braak_embed[braak_stages][..., None]
        q = query + bias
        attn = jnp.einsum('bsd,btd->bst', q, key)
        attn = jax.nn.softmax(attn, axis=-1)
        return jnp.einsum('bst,btd->bsd', attn, value)
    x = x + _L0_cond_ref(x, L0_cond_W1, L0_cond_b1, L0_cond_v, itok_B_0_2)
    x = x + _L1_cond_ref(x, itok_B_0_7, L1_cond_weight, L1_cond_bias)
    x = x + _L2_cond_ref(x, itok_B_0_2, L2_cond_wi, L2_cond_wo, L2_cond_swi, L2_cond_swo, L2_cond_g1, L2_cond_g2)
    x = x + _L3_cond_ref(x, fside_BxSxS_0, fside_BxSxS_0, L3_cond_braak_embed, itok_B_0_5)
    return x

_drawn_inputs = setup_inputs


def setup_inputs(seed=0):
    import zlib

    import numpy as np

    out = dict(_drawn_inputs(seed))
    spreads = {}
    factors = {'L0_cond_b1': 200.0, 'L2_cond_g1': 8.0, 'L2_cond_g2': 8.0, 'L0_cond_v': 2.671}
    for name, (base, spread) in spreads.items():
        noise = np.random.default_rng([zlib.crc32(name.encode()), seed]).standard_normal(out[name].shape)
        drawn = base * np.exp(spread * noise) if base else spread * noise
        out[name] = jnp.asarray(drawn.astype(out[name].dtype))
    for name, factor in factors.items():
        out[name] = (out[name] * factor).astype(out[name].dtype)
    return out
```

```python
from contextlib import ExitStack

import concourse.bass as bass
from concourse import mybir

F32 = mybir.dt.float32
F32R = mybir.dt.float32r
BF16 = mybir.dt.bfloat16
I32 = mybir.dt.int32
ALU = mybir.AluOpType
ACT = mybir.ActivationFunctionType
AX = mybir.AxisListType.X

GS = 4
NEG = -1e30


class Group:

    def __init__(self, number, slot, turn):
        self.n, self.p, self.turn = number, slot, turn
        self.first = isinstance(number, int) and number == 0
        self.fresh = isinstance(turn, int) and turn == 0


def fixed(n):
    return Group(n, n % 2, n // 2)


def looped(i, off):
    return Group(i * 2 + off, off % 2, i + off // 2)


def build(nc, x, tok_mask, tok_subj, side, tok_stage, w1, b1, v, subj_w, subj_b, wi, wo, swi, swo, g1, g2, embed, out):
    B, S, D = x.shape
    A = w1.shape[1]
    NSUB = subj_w.shape[0]
    NEXP, _, F = wi.shape
    NSTAGE = embed.shape[0]
    NSH = swi.shape[0]
    FC = F // 128
    NG = B // GS
    EX = 1 + NSH
    CH = EX * FC
    NH = 3
    N = GS * S
    assert S == 128 and D == 128 and GS * A == 128 and NG % 2 == 0 and N == 512

    with ExitStack() as ctx:
        def sb(name, shape, dt=F32):
            return ctx.enter_context(nc.sbuf_tensor(name, shape, dt))

        def sem(name):
            return ctx.enter_context(nc.semaphore(name))

        def sems(name, n=2):
            return [sem(f"{name}{i}") for i in range(n)]

        ident = sb("ident", [128, 128])
        identb = sb("identb", [128, 128], BF16)
        ones = sb("ones", [128, 128])
        masks = sb("masks", [128, NEXP, S], BF16)
        toks = sb("toks", [1, 3, B], I32)
        tokb = sb("tokb", [128, 2, B], I32)
        tokf = sb("tokf", [128, 2, B])
        row_i = sb("row_i", [128, 1], I32)
        row = sb("row", [128, 1])
        is0 = sb("is0", [128, B])
        is1 = sb("is1", [128, B])
        up = sb("up", [128, 1])
        down = sb("down", [128, 1])
        cnt = sb("cnt", [128, B])
        onehot = sb("onehot", [NSUB, B])
        bias_rows = sb("bias_rows", [NSUB, D])
        bias = sb("bias", [128, B])
        w1p = sb("w1p", [128, GS, 128])
        b1c = sb("b1c", [128, 1])
        vcol = sb("vcol", [128, 1])
        vp = sb("vp", [128, GS, 128])
        subj_in = sb("subj_in", [128, NSUB, D])
        subj_t = sb("subj_t", [128, NSUB, D])
        swi_in = sb("swi_in", [128, NSH, F])
        swi_h = sb("swi_h", [128, NSH, F], F32R)
        swi_l = sb("swi_l", [128, NSH, F], F32R)
        swo_in = sb("swo_in", [128, NSH, FC, D])
        swo_h = sb("swo_h", [128, NSH, FC, D], F32R)
        swo_l = sb("swo_l", [128, NSH, FC, D], F32R)
        g1_sb = sb("g1_sb", [128, EX, D])
        g2_sb = sb("g2_sb", [128, EX])

        x_in = [sb(f"x_in{p}", [128, GS, D]) for p in range(2)]
        mask_in = [sb(f"mask_in{p}", [128, GS, S], BF16) for p in range(2)]
        wsub = [sb(f"wsub{p}", [128, GS, D]) for p in range(2)]
        wi_in = [sb(f"wi_in{p}", [128, GS, F]) for p in range(2)]
        wo_in = [sb(f"wo_in{p}", [128, GS, FC, D]) for p in range(2)]
        side_in = [sb(f"side_in{p}", [128, GS, D]) for p in range(2)]
        emb_in = [sb(f"emb_in{p}", [128, GS, S]) for p in range(2)]
        x2t = [sb(f"x2t{p}", [128, GS, S]) for p in range(2)]
        x2h = [sb(f"x2h{p}", [128, N], F32R) for p in range(2)]
        x2l = [sb(f"x2l{p}", [128, N], F32R) for p in range(2)]
        out_sb = sb("out_sb", [128, B, D])
        xt = sb("xt", [128, GS, S])
        th = sb("th", [128, S])
        nmax1 = sb("nmax1", [128, GS])
        sum1 = sb("sum1", [128, GS])
        den1 = sb("den1", [128, GS])
        rec1 = sb("rec1", [128, GS])
        p1 = sb("p1", [128, GS, S])
        pn = sb("pn", [128, GS, S])
        pnt = sb("pnt", [128, GS, S])
        x1t = sb("x1t", [128, GS, S])
        h_sel = [sb(f"h_sel{i}", [128, GS, S]) for i in range(NH)]
        h_hi = [sb(f"h_hi{i}", [128, N], F32R) for i in range(NH)]
        h_lo = [sb(f"h_lo{i}", [128, N], F32R) for i in range(NH)]
        eo = sb("eo", [128, EX, GS, S])
        gprod = sb("gprod", [128, GS, EX])
        gnmax = sb("gnmax", [128, GS])
        gsh = sb("gsh", [128, GS, EX])
        gexp = sb("gexp", [128, GS, EX])
        gsum = sb("gsum", [128, GS])
        grec = sb("grec", [128, GS])
        gw = sb("gw", [128, GS, EX])
        x3t = sb("x3t", [128, GS, S])
        kt = sb("kt", [128, GS, S])
        qt = sb("qt", [128, GS, S])
        x3n = sb("x3n", [128, GS, D])
        nmax2 = sb("nmax2", [128, GS])
        sum2 = sb("sum2", [128, GS])
        rec2 = sb("rec2", [128, GS])
        p2 = sb("p2", [128, GS, S])
        p2t = sb("p2t", [128, GS, S])

        def bank(name):
            return ctx.enter_context(nc.psum_tensor(name, [128, GS, S], F32))

        fb = bank("fb")
        kb = bank("kb")
        gb = bank("gb")
        hb = [bank(f"hb{i}") for i in range(NH)]
        ab = [bank(f"ab{i}") for i in range(2)]

        ld_tok, ld_w1, ld_subj, ld_small, ld_swi, ld_swo, ld_gate = (
            sem(n) for n in ("ld_tok", "ld_w1", "ld_subj", "ld_small", "ld_swi", "ld_swo", "ld_gate"))
        ld_x, ld_mask, ld_wsub, ld_wi, ld_wo, ld_side, ld_emb = (
            sems(n) for n in ("ld_x", "ld_mask", "ld_wsub", "ld_wi", "ld_wo", "ld_side", "ld_emb"))
        st_out = sem("st_out")
        pool_set, masks_set, ident_set, tok_set, cnt_set, w1p_zero, vp_zero, vp_set, onehot_set = (
            sem(n) for n in ("pool_set", "masks_set", "ident_set", "tok_set", "cnt_set", "w1p_zero", "vp_zero",
                             "vp_set", "onehot_set"))
        bias_ps, bias_set, subj_ps, subj_set, sw_hi, sw_lo = (
            sem(n) for n in ("bias_ps", "bias_set", "subj_ps", "subj_set", "sw_hi", "sw_lo"))
        xt_ps, xt_sb, z_ps, th_sb, sc_ps, nmax1_sb, p1_sb, den1_sb, rec1_sb, pn_sb = (
            sem(n) for n in ("xt_ps", "xt_sb", "z_ps", "th_sb", "sc_ps", "nmax1_sb", "p1_sb", "den1_sb", "rec1_sb",
                             "pn_sb"))
        pnt_ps, pnt_sb, x1_ps, x1_sb, x2_ps, x2_sb, x2h_sb, x2l_sb = (
            sem(n) for n in ("pnt_ps", "pnt_sb", "x1_ps", "x1_sb", "x2_ps", "x2_sb", "x2h_sb", "x2l_sb"))
        h_ps, h_sb, hl_sb, hid_used, eo_sb = (sem(n) for n in ("h_ps", "h_sb", "hl_sb", "hid_used", "eo_sb"))
        g1_ps, gprod_sb, g2_ps, gnmax_sb, gsh_sb, gexp_sb, gsum_sb, grec_sb, gw_sb, x3_sb = (
            sem(n) for n in ("g1_ps", "gprod_sb", "g2_ps", "gnmax_sb", "gsh_sb", "gexp_sb", "gsum_sb", "grec_sb",
                             "gw_sb", "x3_sb"))
        kt_ps, kt_sb, qt_sb, x3n_ps, x3n_sb, at_ps, nmax2_sb, p2_sb, rec2_sb, p2t_ps, p2t_sb, pv_ps, out_rdy = (
            sem(n) for n in ("kt_ps", "kt_sb", "qt_sb", "x3n_ps", "x3n_sb", "at_ps", "nmax2_sb", "p2_sb", "rec2_sb",
                             "p2t_ps", "p2t_sb", "pv_ps", "out_rdy"))

        def flat(t):
            return t[:].rearrange("p b s -> p (b s)")

        def acc_of(g, e):
            return ab[(EX * g.p + e) % 2]

        def pipeline(eng, front, step, back, peeled=0):
            front(fixed(0))
            step(None, fixed(0), fixed(1))
            with eng.Fori(0, (NG - 2 - peeled) // 2) as i:
                for u in range(2):
                    step(looped(i, u), looped(i, u + 1), looped(i, u + 2))
            for g in range(NG - 1 - peeled, NG - 1):
                step(fixed(g - 1), fixed(g), fixed(g + 1))
            step(fixed(NG - 2), fixed(NG - 1), None)
            back(fixed(NG - 1))

        block = ctx.enter_context(nc.Block())

        @block.sync
        def _(sp):
            def picks(g, row, count):
                return [sp.value_load(toks[0:1, row, bass.ds(g.n * GS + b, 1)], min_val=0, max_val=count - 1)
                        for b in range(GS)]

            def load_front(g):
                kinds, subjs = picks(g, 0, NEXP), picks(g, 1, NSUB)
                if not g.fresh:
                    sp.wait_ge(x2_ps, g.n - 1)
                sp.dma_start(x_in[g.p][:], x[bass.ds(g.n * GS, GS)].rearrange("b s d -> s b d")).then_inc(ld_x[g.p], 16)
                for b in range(GS):
                    sp.dma_start(mask_in[g.p][:, b, :], masks[:, bass.ds(kinds[b], 1), :]).then_inc(ld_mask[g.p], 16)
                for b in range(GS):
                    sp.dma_start(wsub[g.p][:, b, :], subj_t[:, bass.ds(subjs[b], 1), :]).then_inc(ld_wsub[g.p], 16)

            def load_mid(g):
                kinds = picks(g, 0, NEXP)
                if not g.fresh:
                    sp.wait_ge(hid_used, CH * (g.n - 2) + FC)
                for b in range(GS):
                    sp.dma_start(wi_in[g.p][:, b, :],
                                 wi[bass.ds(kinds[b], 1)].rearrange("o d f -> d (o f)")).then_inc(ld_wi[g.p], 16)
                for b in range(GS):
                    sp.dma_start(wo_in[g.p][:, b, :, :],
                                 wo[bass.ds(kinds[b], 1)].rearrange("o (c f) d -> f (o c) d", c=FC)).then_inc(ld_wo[g.p], 16)

            def load_back(g):
                stages = picks(g, 2, NSTAGE)
                if not g.fresh or not isinstance(g.n, int):
                    sp.wait_ge(h_ps, CH * g.n + 1)
                sp.dma_start(side_in[g.p][:],
                             side[bass.ds(g.n * GS, GS)].rearrange("b s d -> s b d")).then_inc(ld_side[g.p], 16)
                for b in range(GS):
                    sp.dma_start(emb_in[g.p][:, b, :],
                                 embed[bass.ds(stages[b], 1)].to_broadcast([128, S])).then_inc(ld_emb[g.p], 16)

            def store(g):
                sp.wait_ge(out_rdy, GS * (g.n + 1))
                sp.dma_start(out[bass.ds(g.n * GS, GS)].rearrange("b s d -> s b d"), out_sb[:, bass.ds(g.n * GS, GS), :]).then_inc(st_out, 16)

            def front(g):
                sp.dma_start(x_in[0][:], x[0:GS].rearrange("b s d -> s b d")).then_inc(ld_x[0], 16)
                for n, t in enumerate((tok_mask, tok_subj, tok_stage)):
                    sp.dma_start(toks[:, n, :], t.rearrange("(a b) -> a b", a=1)).then_inc(ld_tok, 16)
                for n, t in enumerate((tok_mask, tok_subj)):
                    sp.dma_start(tokb[:, n, :], t.rearrange("(a b) -> a b", a=1).to_broadcast([128, B])).then_inc(ld_tok, 16)
                sp.dma_start(subj_in[:], subj_w.rearrange("s o h -> o s h")).then_inc(ld_subj, 16)
                sp.wait_ge(ld_tok, 80)
                load_mid(g)
                sp.wait_ge(masks_set, 3)
                for b in range(GS):
                    kind = sp.value_load(toks[0:1, 0, b:b + 1], min_val=0, max_val=NEXP - 1)
                    sp.dma_start(mask_in[0][:, b, :], masks[:, bass.ds(kind, 1), :]).then_inc(ld_mask[0], 16)
                sp.wait_ge(subj_set, 2)
                for b in range(GS):
                    subj = sp.value_load(toks[0:1, 1, b:b + 1], min_val=0, max_val=NSUB - 1)
                    sp.dma_start(wsub[0][:, b, :], subj_t[:, bass.ds(subj, 1), :]).then_inc(ld_wsub[0], 16)
                sp.dma_start(swi_in[:], swi.rearrange("e d f -> d e f")).then_inc(ld_swi, 16)
                sp.dma_start(swo_in[:], swo.rearrange("e (c f) d -> f e c d", c=FC)).then_inc(ld_swo, 16)
                sp.dma_start(g1_sb[:], g1.rearrange("(c k) d -> k c d", c=EX)).then_inc(ld_gate, 16)
                sp.dma_start(g2_sb[:], g2).then_inc(ld_gate, 16)
                load_front(fixed(1))

            def step(gb_, gm, gf):
                if gf is not None:
                    load_mid(gf)
                load_back(gm)
                if gf is not None and not (isinstance(gf.n, int) and gf.n == NG - 1):
                    load_front(Group(gf.n + 1, 1 - gf.p, gf.turn + gf.p))
                if gb_ is not None:
                    store(gb_)

            pipeline(sp, front, step, store, peeled=2)
            sp.wait_ge(st_out, 16 * NG)

        @block.gpsimd
        def _(pool):
            nc.gpsimd.memset(ident[:], 0.0).then_inc(pool_set, 1)
            nc.gpsimd.memset(masks[:], 0.0).then_inc(pool_set, 1)
            nc.gpsimd.iota(row_i[:], pattern=[[0, 1]], base=0, channel_multiplier=1).then_inc(pool_set, 1)
            nc.gpsimd.memset(ones[:], 1.0).then_inc(pool_set, 1)
            pool.wait_ge(pool_set, 4)
            nc.gpsimd.affine_select(out=ident[:], in_=ident[:], compare_op=ALU.not_equal, fill=1.0, base=0,
                                    pattern=[[-1, 128]], channel_multiplier=1).then_inc(ident_set, 1)
            nc.gpsimd.affine_select(out=masks[:, 0, :], in_=masks[:, 0, :], compare_op=ALU.is_ge, fill=NEG, base=0,
                                    pattern=[[-1, S]], channel_multiplier=1).then_inc(masks_set, 1)
            nc.gpsimd.affine_select(out=masks[:, 1, :], in_=masks[:, 1, :], compare_op=ALU.is_ge, fill=NEG, base=0,
                                    pattern=[[1, S]], channel_multiplier=-1).then_inc(masks_set, 1)
            nc.gpsimd.affine_select(out=masks[:, 2:NEXP, :], in_=masks[:, 2:NEXP, :], compare_op=ALU.not_equal,
                                    fill=NEG, base=0, pattern=[[0, NEXP - 2], [-1, S]],
                                    channel_multiplier=1).then_inc(masks_set, 1)

            def split_x2(g):
                pool.wait_ge(x2h_sb, g.n + 1)
                if not g.fresh:
                    pool.wait_ge(h_ps, CH * (g.n - 1))
                nc.gpsimd.tensor_tensor(x2l[g.p][:], flat(x2t[g.p]), x2h[g.p][:].bitcast(F32),
                                        ALU.subtract).then_inc(x2l_sb, 1)

            def query(g):
                pool.wait_ge(x3_sb, EX * GS * (g.n + 1))
                pool.wait_ge(ld_emb[g.p], 16 * GS * (g.turn + 1))
                nc.gpsimd.tensor_tensor(qt[:], x3t[:], emb_in[g.p][:], ALU.add).then_inc(qt_sb, 1)

            def step(gb_, gm, gf):
                if gb_ is not None:
                    query(gb_)
                if gf is not None:
                    split_x2(gf)

            pipeline(pool, split_x2, step, query)

        @block.scalar
        def _(act):
            act.dma_start(bias_rows[:], subj_b).then_inc(ld_small, 16)
            for b in range(GS):
                act.dma_start(b1c[b * A:(b + 1) * A, :], b1.rearrange("(a o) -> a o", o=1)).then_inc(ld_small, 16)
                act.dma_start(vcol[b * A:(b + 1) * A, :], v.rearrange("(a o) -> a o", o=1)).then_inc(ld_small, 16)
            act.wait_ge(w1p_zero, 1)
            for b in range(GS):
                act.dma_start(w1p[:, b, b * A:(b + 1) * A], w1).then_inc(ld_w1, 16)

            def copy_xt(g):
                act.wait_ge(xt_ps, g.n + 1)
                nc.scalar.copy(flat(xt), flat(fb)).then_inc(xt_sb, 1)

            def tanh(g):
                act.wait_ge(z_ps, g.n + 1)
                nc.scalar.activation(th[:], fb[:, 0, :], ACT.Tanh, bias=b1c[:, 0:1]).then_inc(th_sb, 1)

            def exp1(g):
                act.wait_ge(nmax1_sb, g.n + 1)
                for b in range(GS):
                    nc.scalar.activation(p1[:, b, :], fb[:, b, :], ACT.Exp, bias=nmax1[:, b:b + 1],
                                         accum_out=sum1[:, b:b + 1]).then_inc(p1_sb, 1)

            def copy_pnt(g):
                act.wait_ge(pnt_ps, g.n + 1)
                nc.scalar.copy(flat(pnt), flat(fb)).then_inc(pnt_sb, 1)

            def copy_x1(g):
                act.wait_ge(x1_ps, g.n + 1)
                nc.scalar.copy(flat(x1t), flat(fb)).then_inc(x1_sb, 1)

            def split_x2(g):
                act.wait_ge(x2_sb, g.n + 1)
                if not g.fresh:
                    act.wait_ge(h_ps, CH * (g.n - 1))
                nc.scalar.activation(x2h[g.p][:], flat(x2t[g.p]), ACT.Identity).then_inc(x2h_sb, 1)

            def hidden(g, c):
                act.wait_ge(h_ps, CH * g.n + c + 1)
                if c >= NH or not g.first:
                    act.wait_ge(hid_used, CH * g.n + c + 1 - NH)
                dst = flat(h_sel[c % NH]) if c < FC else h_hi[c % NH][:]
                nc.scalar.activation(dst, flat(hb[c % NH]), ACT.Relu).then_inc(h_sb, 1)

            def expert_out(g, e):
                act.wait_ge(hid_used, CH * g.n + FC * (e + 1))
                if not g.first:
                    act.wait_ge(x3_sb, EX * GS * g.n)
                nc.scalar.copy(eo[:, e].rearrange("p b s -> p (b s)"), flat(acc_of(g, e))).then_inc(eo_sb, 1)

            def gate(g):
                act.wait_ge(gsh_sb, g.n + 1)
                nc.scalar.activation(gexp[:], gsh[:], ACT.Exp).then_inc(gexp_sb, 1)

            def copy_kt(g):
                act.wait_ge(kt_ps, g.n + 1)
                nc.scalar.copy(flat(kt), flat(kb)).then_inc(kt_sb, 1)

            def copy_x3n(g):
                act.wait_ge(x3n_ps, g.n + 1)
                nc.scalar.copy(flat(x3n), flat(kb)).then_inc(x3n_sb, 1)

            def exp2(g):
                act.wait_ge(nmax2_sb, g.n + 1)
                for b in range(GS):
                    nc.scalar.activation(p2[:, b, :], kb[:, b, :], ACT.Exp, bias=nmax2[:, b:b + 1],
                                         accum_out=sum2[:, b:b + 1]).then_inc(p2_sb, 1)

            def copy_p2t(g):
                act.wait_ge(p2t_ps, g.n + 1)
                nc.scalar.copy(flat(p2t), flat(kb)).then_inc(p2t_sb, 1)

            def front(g):
                act.wait_ge(ld_small, 16 * (1 + 2 * GS))
                copy_xt(g)
                tanh(g)
                exp1(g)
                copy_pnt(g)
                copy_x1(g)
                split_x2(g)
                act.wait_ge(ld_swi, 16)
                nc.scalar.activation(swi_h[:], swi_in[:], ACT.Identity).then_inc(sw_hi, 1)
                act.wait_ge(ld_swo, 16)
                nc.scalar.activation(swo_h[:], swo_in[:], ACT.Identity).then_inc(sw_hi, 1)

            def step(gb_, gm, gf):
                for c in range(CH):
                    hidden(gm, c)
                    if c % FC == 2 and c > FC:
                        expert_out(gm, c // FC - 1)
                    if gb_ is not None:
                        if c == 1:
                            gate(gb_)
                            copy_kt(gb_)
                        if c == 4:
                            copy_x3n(gb_)
                        if c == 6:
                            exp2(gb_)
                        if c == 8:
                            copy_p2t(gb_)
                    if gf is not None:
                        if c == 0:
                            copy_xt(gf)
                        if c == 2:
                            tanh(gf)
                        if c == 3:
                            exp1(gf)
                        if c == 5:
                            copy_pnt(gf)
                        if c == 7:
                            copy_x1(gf)
                        if c == 9:
                            split_x2(gf)
                expert_out(gm, EX - 1)

            def back(g):
                gate(g)
                copy_kt(g)
                copy_x3n(g)
                exp2(g)
                copy_p2t(g)

            pipeline(act, front, step, back)

        @block.vector
        def _(dve):
            def setup():
                nc.vector.memset(w1p[:], 0.0).then_inc(w1p_zero, 1)
                nc.vector.memset(vp[:], 0.0).then_inc(vp_zero, 1)
                dve.wait_ge(ident_set, 1)
                nc.vector.tensor_copy(identb[:], ident[:]).then_inc(ident_set, 1)
                nc.vector.tensor_copy(row[:], row_i[:]).then_inc(tok_set, 1)
                dve.wait_ge(vp_zero, 1)
                dve.wait_ge(ld_small, 16 * (1 + 2 * GS))
                for b in range(GS):
                    rows = slice(b * A, (b + 1) * A)
                    nc.vector.tensor_scalar(vp[rows, b, :], vp[rows, b, :], vcol[rows, 0:1], None,
                                            ALU.add).then_inc(vp_set, 1)
                dve.wait_ge(ld_tok, 80)
                nc.vector.tensor_copy(tokf[:], tokb[:]).then_inc(tok_set, 1)
                dve.wait_ge(tok_set, 2)
                nc.vector.tensor_scalar(onehot[:], tokf[0:NSUB, 1, :], row[0:NSUB, 0:1], None,
                                        ALU.is_equal).then_inc(onehot_set, 1)
                nc.vector.tensor_scalar(is0[:], tokf[:, 0, :], 0.0, None, ALU.is_equal).then_inc(cnt_set, 1)
                nc.vector.tensor_scalar(is1[:], tokf[:, 0, :], 1.0, None, ALU.is_equal).then_inc(cnt_set, 1)
                nc.vector.tensor_scalar(up[:], row[:], 1.0, float(2 - S), ALU.mult, ALU.add).then_inc(cnt_set, 1)
                nc.vector.tensor_scalar(down[:], row[:], -1.0, 1.0, ALU.mult, ALU.add).then_inc(cnt_set, 1)
                dve.wait_ge(cnt_set, 4)
                nc.vector.tensor_scalar(cnt[:], is0[:], up[:, 0:1], float(S - 1), ALU.mult, ALU.add).then_inc(cnt_set, 1)
                dve.wait_ge(cnt_set, 5)
                nc.vector.scalar_tensor_tensor(out=cnt[:], in0=is1[:], scalar=down[:, 0:1], in1=cnt[:],
                                               op0=ALU.mult, op1=ALU.add).then_inc(cnt_set, 1)
                for n in range(2):
                    dve.wait_ge(subj_ps, n + 1)
                    half = slice(n * NSUB // 2, (n + 1) * NSUB // 2)
                    nc.vector.tensor_tensor(subj_t[:, half, :], hb[n][:],
                                            ident[:].rearrange("p (o s) -> p o s", o=1).to_broadcast([128, GS, S]),
                                            ALU.add).then_inc(subj_set, 1)
                dve.wait_ge(bias_ps, 1)
                nc.vector.tensor_copy(bias[:], gb[:, 0, 0:B]).then_inc(bias_set, 1)

            def max1(g):
                dve.wait_ge(sc_ps, g.n + 1)
                nc.vector.tensor_reduce(nmax1[:], fb[:], AX, ALU.max, negate=True).then_inc(nmax1_sb, 1)

            def norm1(g):
                dve.wait_ge(p1_sb, GS * (g.n + 1))
                nc.vector.tensor_tensor(den1[:], sum1[:], cnt[:, bass.ds(g.n * GS, GS)], ALU.mult).then_inc(den1_sb, 1)
                dve.wait_ge(den1_sb, g.n + 1)
                nc.vector.reciprocal(rec1[:], den1[:]).then_inc(rec1_sb, 1)
                dve.wait_ge(rec1_sb, g.n + 1)
                for b in range(GS):
                    nc.vector.scalar_tensor_tensor(out=pn[:, b, :], in0=p1[:, b, :], scalar=rec1[:, b:b + 1],
                                                   in1=ident[:], op0=ALU.mult, op1=ALU.add).then_inc(pn_sb, 1)

            def add_bias(g):
                dve.wait_ge(x2_ps, g.n + 1)
                if not g.fresh:
                    dve.wait_ge(x3_sb, EX * GS * (g.n - 1))
                nc.vector.tensor_tensor(x2t[g.p][:], fb[:],
                                        bias[:, bass.ds(g.n * GS, GS)].rearrange("p (b o) -> p b o", o=1)
                                        .to_broadcast([128, GS, S]), ALU.add).then_inc(x2_sb, 1)

            def hidden_low(g, c):
                dve.wait_ge(h_sb, CH * g.n + c + 1)
                nc.vector.scalar_tensor_tensor(out=h_lo[c % NH][:], in0=flat(hb[c % NH]), scalar=0.0,
                                               in1=h_hi[c % NH][:].bitcast(F32), op0=ALU.max,
                                               op1=ALU.subtract).then_inc(hl_sb, 1)

            def gate1(g):
                dve.wait_ge(g1_ps, g.n + 1)
                nc.vector.scalar_tensor_tensor(
                    out=gprod[:], in0=gb[:, 0, 0:GS].rearrange("p (b o) -> p b o", o=1).to_broadcast([128, GS, EX]),
                    scalar=0.0, in1=g2_sb[:].rearrange("p (o e) -> p o e", o=1).to_broadcast([128, GS, EX]),
                    op0=ALU.max, op1=ALU.mult).then_inc(gprod_sb, 1)

            def gate2(g):
                dve.wait_ge(g2_ps, g.n + 1)
                logits = gb[:, 1, 0:GS * EX].rearrange("p (b e) -> p b e", e=EX)
                nc.vector.tensor_reduce(gnmax[:], logits, AX, ALU.max, negate=True).then_inc(gnmax_sb, 1)
                dve.wait_ge(gnmax_sb, g.n + 1)
                nc.vector.tensor_tensor(gsh[:], logits, gnmax[:].rearrange("p (b o) -> p b o", o=1)
                                        .to_broadcast([128, GS, EX]), ALU.add).then_inc(gsh_sb, 1)

            def gate3(g):
                dve.wait_ge(gexp_sb, g.n + 1)
                nc.vector.tensor_reduce(gsum[:], gexp[:], AX, ALU.add).then_inc(gsum_sb, 1)
                dve.wait_ge(gsum_sb, g.n + 1)
                nc.vector.reciprocal(grec[:], gsum[:]).then_inc(grec_sb, 1)
                dve.wait_ge(grec_sb, g.n + 1)
                nc.vector.tensor_tensor(gw[:], gexp[:], grec[:].rearrange("p (b o) -> p b o", o=1)
                                        .to_broadcast([128, GS, EX]), ALU.mult).then_inc(gw_sb, 1)
                dve.wait_ge(gw_sb, g.n + 1)
                for e in range(EX):
                    for b in range(GS):
                        if e:
                            dve.wait_ge(x3_sb, EX * GS * g.n + GS * (e - 1) + b + 1)
                        nc.vector.scalar_tensor_tensor(out=x3t[:, b, :], in0=eo[:, e, b, :], scalar=gw[:, b, e:e + 1],
                                                       in1=(x3t if e else x2t[g.p])[:, b, :], op0=ALU.mult,
                                                       op1=ALU.add).then_inc(x3_sb, 1)

            def max2(g):
                dve.wait_ge(at_ps, g.n + 1)
                nc.vector.tensor_reduce(nmax2[:], kb[:], AX, ALU.max, negate=True).then_inc(nmax2_sb, 1)

            def norm2(g):
                dve.wait_ge(p2_sb, GS * (g.n + 1))
                nc.vector.reciprocal(rec2[:], sum2[:]).then_inc(rec2_sb, 1)

            def result(g):
                dve.wait_ge(pv_ps, g.n + 1)
                dve.wait_ge(x3n_sb, g.n + 1)
                dve.wait_ge(rec2_sb, g.n + 1)
                for b in range(GS):
                    nc.vector.scalar_tensor_tensor(out=out_sb[:, bass.ds(g.n * GS + b, 1), :], in0=kb[:, b, :], scalar=rec2[:, b:b + 1],
                                                   in1=x3n[:, b, :], op0=ALU.mult, op1=ALU.add).then_inc(out_rdy, 1)

            def front(g):
                setup()
                max1(g)
                norm1(g)
                add_bias(g)
                dve.wait_ge(sw_hi, 1)
                nc.vector.tensor_tensor(swi_l[:], swi_in[:], swi_h[:].bitcast(F32), ALU.subtract).then_inc(sw_lo, 1)
                dve.wait_ge(sw_hi, 2)
                nc.vector.tensor_tensor(swo_l[:], swo_in[:], swo_h[:].bitcast(F32), ALU.subtract).then_inc(sw_lo, 1)

            def step(gb_, gm, gf):
                for c in range(CH):
                    if c >= FC:
                        hidden_low(gm, c)
                    if gb_ is not None:
                        if c == 0:
                            gate1(gb_)
                        if c == 1:
                            gate2(gb_)
                            gate3(gb_)
                        if c == 5:
                            max2(gb_)
                        if c == 7:
                            norm2(gb_)
                        if c == 10:
                            result(gb_)
                    if gf is not None:
                        if c == 2:
                            max1(gf)
                        if c == 4:
                            norm1(gf)
                        if c == 8:
                            add_bias(gf)

            def back(g):
                gate1(g)
                gate2(g)
                gate3(g)
                max2(g)
                norm2(g)
                result(g)

            pipeline(dve, front, step, back)

        @block.tensor
        def _(pe):
            def setup():
                pe.wait_ge(ident_set, 2)
                pe.wait_ge(ld_subj, 16)
                for n in range(NSUB):
                    t = nc.tensor.transpose(hb[n // GS][:, n % GS, :], subj_in[:, n, :], ident[:])
                    if n % GS == GS - 1:
                        t.then_inc(subj_ps, 1)
                pe.wait_ge(onehot_set, 1)
                pe.wait_ge(ld_small, 16 * (1 + 2 * GS))
                nc.tensor.matmul(gb[:, 0, 0:B], bias_rows[:], onehot[:], start=True, stop=True).then_inc(bias_ps, 1)

            def x_turn(g):
                pe.wait_ge(ld_x[g.p], 16 * (g.turn + 1))
                if not g.first:
                    pe.wait_ge(x2_sb, g.n)
                for b in range(GS):
                    t = nc.tensor.transpose(fb[:, b, :], x_in[g.p][:, b, :], ident[:])
                t.then_inc(xt_ps, 1)

            def z(g):
                pe.wait_ge(xt_sb, g.n + 1)
                for b in range(GS):
                    m = nc.tensor.matmul(fb[:, 0, :], w1p[:, b, :], xt[:, b, :], start=b == 0, stop=b == GS - 1)
                m.then_inc(z_ps, 1)

            def scores1(g):
                pe.wait_ge(th_sb, g.n + 1)
                pe.wait_ge(ld_mask[g.p], 16 * GS * (g.turn + 1))
                for b in range(GS):
                    nc.tensor.matmul(fb[:, b, :], identb[:], mask_in[g.p][:, b, :], start=True, stop=False)
                    m = nc.tensor.matmul(fb[:, b, :], vp[:, b, :], th[:], start=False, stop=True)
                m.then_inc(sc_ps, 1)

            def pn_turn(g):
                pe.wait_ge(pn_sb, GS * (g.n + 1))
                for b in range(GS):
                    t = nc.tensor.transpose(fb[:, b, :], pn[:, b, :], ident[:])
                t.then_inc(pnt_ps, 1)

            def pooled(g):
                pe.wait_ge(pnt_sb, g.n + 1)
                for b in range(GS):
                    m = nc.tensor.matmul(fb[:, b, :], x_in[g.p][:, b, :], pnt[:, b, :], start=True, stop=True)
                m.then_inc(x1_ps, 1)

            def subject(g):
                pe.wait_ge(x1_sb, g.n + 1)
                pe.wait_ge(ld_wsub[g.p], 16 * GS * (g.turn + 1))
                for b in range(GS):
                    m = nc.tensor.matmul(fb[:, b, :], wsub[g.p][:, b, :], x1t[:, b, :], start=True, stop=True)
                m.then_inc(x2_ps, 1)

            def hid(g, c):
                e, k = c // FC, c % FC
                cols = slice(k * 128, (k + 1) * 128)
                dst = hb[c % NH]
                if c >= NH or not g.first:
                    pe.wait_ge(h_sb, CH * g.n + c + 1 - NH)
                    if c >= NH + FC:
                        pe.wait_ge(hl_sb, (CH - FC) * g.n + c + 1 - NH - FC)
                    elif c < NH:
                        pe.wait_ge(hl_sb, (CH - FC) * g.n + c + 1 - NH)
                if e == 0:
                    if k == 0:
                        pe.wait_ge(x2_sb, g.n + 1)
                        pe.wait_ge(ld_wi[g.p], 16 * GS * (g.turn + 1))
                    for b in range(GS):
                        m = nc.tensor.matmul(dst[:, b, :], wi_in[g.p][:, b, cols], x2t[g.p][:, b, :],
                                             start=True, stop=True)
                else:
                    if e == 1 and k == 0:
                        pe.wait_ge(x2l_sb, g.n + 1)
                        if g.first:
                            pe.wait_ge(sw_lo, 1)
                    nc.tensor.matmul(flat(dst), swi_h[:, e - 1, cols], x2h[g.p][:], start=True, stop=False)
                    nc.tensor.matmul(flat(dst), swi_h[:, e - 1, cols], x2l[g.p][:], start=False, stop=False)
                    m = nc.tensor.matmul(flat(dst), swi_l[:, e - 1, cols], x2h[g.p][:], start=False, stop=True)
                m.then_inc(h_ps, 1)

            def outp(g, c):
                e, k = c // FC, c % FC
                acc = acc_of(g, e)
                if k == 0 and (e >= 2 or not g.first):
                    pe.wait_ge(eo_sb, EX * g.n + e - 1)
                if e == 0:
                    pe.wait_ge(h_sb, CH * g.n + c + 1)
                    if k == 0:
                        pe.wait_ge(ld_wo[g.p], 16 * GS * (g.turn + 1))
                    for b in range(GS):
                        m = nc.tensor.matmul(acc[:, b, :], wo_in[g.p][:, b, k, :], h_sel[c % NH][:, b, :],
                                             start=k == 0 and b == 0, stop=k == FC - 1, skip_group_check=True)
                else:
                    if e == 1 and k == 0 and g.first:
                        pe.wait_ge(sw_lo, 2)
                    pe.wait_ge(hl_sb, (CH - FC) * g.n + c + 1 - FC)
                    hh, hl = h_hi[c % NH][:], h_lo[c % NH][:]
                    nc.tensor.matmul(flat(acc), swo_h[:, e - 1, k, :], hh, start=k == 0, stop=False)
                    nc.tensor.matmul(flat(acc), swo_l[:, e - 1, k, :], hh, start=False, stop=False)
                    m = nc.tensor.matmul(flat(acc), swo_h[:, e - 1, k, :], hl, start=False, stop=k == FC - 1)
                m.then_inc(hid_used, 1)

            def gate1(g):
                pe.wait_ge(eo_sb, EX * (g.n + 1))
                if g.first:
                    pe.wait_ge(ld_gate, 32)
                    pe.wait_ge(bias_set, 1)
                for e in range(EX):
                    m = nc.tensor.matmul(gb[:, 0, 0:GS], g1_sb[:, e, :], eo[:, e, :, 0], start=e == 0, stop=e == EX - 1)
                m.then_inc(g1_ps, 1)

            def gate2(g):
                pe.wait_ge(gprod_sb, g.n + 1)
                nc.tensor.matmul(gb[:, 1, 0:GS * EX], ones[:], gprod[:].rearrange("p b e -> p (b e)"),
                                 start=True, stop=True).then_inc(g2_ps, 1)

            def key_turn(g):
                pe.wait_ge(ld_side[g.p], 16 * (g.turn + 1))
                for b in range(GS):
                    t = nc.tensor.transpose(kb[:, b, :], side_in[g.p][:, b, :], ident[:])
                t.then_inc(kt_ps, 1)

            def x3_turn(g):
                pe.wait_ge(x3_sb, EX * GS * (g.n + 1))
                pe.wait_ge(kt_sb, g.n + 1)
                for b in range(GS):
                    t = nc.tensor.transpose(kb[:, b, :], x3t[:, b, :], ident[:])
                t.then_inc(x3n_ps, 1)

            def scores2(g):
                pe.wait_ge(qt_sb, g.n + 1)
                pe.wait_ge(x3n_sb, g.n + 1)
                for b in range(GS):
                    m = nc.tensor.matmul(kb[:, b, :], qt[:, b, :], kt[:, b, :], start=True, stop=True)
                m.then_inc(at_ps, 1)

            def p2_turn(g):
                pe.wait_ge(p2_sb, GS * (g.n + 1))
                for b in range(GS):
                    t = nc.tensor.transpose(kb[:, b, :], p2[:, b, :], ident[:])
                t.then_inc(p2t_ps, 1)

            def attend(g):
                pe.wait_ge(p2t_sb, g.n + 1)
                for b in range(GS):
                    m = nc.tensor.matmul(kb[:, b, :], p2t[:, b, :], side_in[g.p][:, b, :], start=True, stop=True)
                m.then_inc(pv_ps, 1)

            def front(g):
                pe.wait_ge(ident_set, 2)
                x_turn(g)
                pe.wait_ge(ld_w1, 16 * GS)
                z(g)
                setup()
                pe.wait_ge(vp_set, GS)
                scores1(g)
                pn_turn(g)
                pooled(g)
                pe.wait_ge(bias_set, 1)
                subject(g)

            def step(gb_, gm, gf):
                for c in range(CH + 2):
                    if c == 0:
                        pe.wait_ge(subj_set, 2)
                    if c < CH:
                        hid(gm, c)
                    if c >= 2:
                        outp(gm, c - 2)
                    if gb_ is not None:
                        if c == 0:
                            gate1(gb_)
                        if c == 1:
                            gate2(gb_)
                            key_turn(gb_)
                        if c == 4:
                            x3_turn(gb_)
                        if c == 5:
                            scores2(gb_)
                        if c == 8:
                            p2_turn(gb_)
                        if c == 9:
                            attend(gb_)
                    if gf is not None:
                        if c == 0:
                            x_turn(gf)
                        if c == 1:
                            z(gf)
                        if c == 2:
                            scores1(gf)
                        if c == 5:
                            pn_turn(gf)
                        if c == 6:
                            pooled(gf)
                        if c == 7:
                            subject(gf)

            def back(g):
                gate1(g)
                gate2(g)
                key_turn(g)
                x3_turn(g)
                scores2(g)
                p2_turn(g)
                attend(g)

            pipeline(pe, front, step, back)


_INS = ["x", "itok_B_0_2", "itok_B_0_7", "fside_BxSxS_0", "itok_B_0_5", "L0_cond_W1", "L0_cond_b1", "L0_cond_v",
        "L1_cond_weight", "L1_cond_bias", "L2_cond_wi", "L2_cond_wo", "L2_cond_swi", "L2_cond_swo", "L2_cond_g1",
        "L2_cond_g2", "L3_cond_braak_embed"]


def kernel(**inputs):
    import concourse.bacc as bacc
    import numpy as np
    from concourse.bass_utils import run_bass_kernel_spmd

    nc = bacc.Bacc("TRN2", target_bir_lowering=False, num_devices=1)
    arrays, args = {}, []
    for name in _INS:
        a = np.ascontiguousarray(inputs[name])
        arrays[f"in_{name}"] = a
        args.append(nc.dram_tensor(f"in_{name}", a.shape, mybir.dt.from_np(a.dtype), kind="ExternalInput").ap())
    out = nc.dram_tensor("out", inputs["x"].shape, F32, kind="ExternalOutput").ap()
    build(nc, *args, out)
    return run_bass_kernel_spmd(nc, [arrays], core_ids=[0]).results[0]["out"]
```

```python
from contextlib import ExitStack

import concourse.bass as bass
from concourse import mybir

F32 = mybir.dt.float32
F32R = mybir.dt.float32r
BF16 = mybir.dt.bfloat16
I32 = mybir.dt.int32
ALU = mybir.AluOpType
ACT = mybir.ActivationFunctionType
AX = mybir.AxisListType.X

GS = 4
NEG = -1e30


class Group:

    def __init__(self, number, slot, turn):
        self.n, self.p, self.turn = number, slot, turn
        self.first = isinstance(number, int) and number == 0
        self.fresh = isinstance(turn, int) and turn == 0


def fixed(n):
    return Group(n, n % 2, n // 2)


def looped(i, off):
    return Group(i * 2 + off, off % 2, i + off // 2)


def build(nc, x, tok_mask, tok_subj, side, tok_stage, w1, b1, v, subj_w, subj_b, wi, wo, swi, swo, g1, g2, embed, out):
    B, S, D = x.shape
    A = w1.shape[1]
    NSUB = subj_w.shape[0]
    NEXP, _, F = wi.shape
    NSTAGE = embed.shape[0]
    NSH = swi.shape[0]
    FC = F // 128
    NG = B // GS
    EX = 1 + NSH
    CH = EX * FC
    NH = 3
    N = GS * S
    assert S == 128 and D == 128 and GS * A == 128 and NG % 2 == 0 and N == 512

    with ExitStack() as ctx:
        def sb(name, shape, dt=F32):
            return ctx.enter_context(nc.sbuf_tensor(name, shape, dt))

        def sem(name):
            return ctx.enter_context(nc.semaphore(name))

        def sems(name, n=2):
            return [sem(f"{name}{i}") for i in range(n)]

        ident = sb("ident", [128, 128])
        identb = sb("identb", [128, 128], BF16)
        ones = sb("ones", [128, 128])
        masks = sb("masks", [128, NEXP, S], BF16)
        toks = sb("toks", [1, 3, B], I32)
        tokb = sb("tokb", [128, 2, B], I32)
        tokf = sb("tokf", [128, 2, B])
        row_i = sb("row_i", [128, 1], I32)
        row = sb("row", [128, 1])
        is0 = sb("is0", [128, B])
        is1 = sb("is1", [128, B])
        up = sb("up", [128, 1])
        down = sb("down", [128, 1])
        cnt = sb("cnt", [128, B])
        onehot = sb("onehot", [NSUB, B])
        bias_rows = sb("bias_rows", [NSUB, D])
        bias = sb("bias", [128, B])
        w1p = sb("w1p", [128, GS, 128])
        w1_in = sb("w1_in", [128, A])
        rows_in = sb("rows_in", [1, 2, A])
        rows_rep = sb("rows_rep", [1, 2, GS, A])
        cols = sb("cols", [128, 2])
        vp = sb("vp", [128, GS, 128])
        subj_in = sb("subj_in", [128, NSUB, D])
        subj_t = sb("subj_t", [128, NSUB, D])
        swi_in = sb("swi_in", [128, NSH, F])
        swi_h = sb("swi_h", [128, NSH, F], F32R)
        swi_l = sb("swi_l", [128, NSH, F], F32R)
        swo_in = sb("swo_in", [128, NSH, FC, D])
        swo_h = sb("swo_h", [128, NSH, FC, D], F32R)
        swo_l = sb("swo_l", [128, NSH, FC, D], F32R)
        g1_sb = sb("g1_sb", [128, EX, D])
        g2_sb = sb("g2_sb", [128, EX])

        x_in = [sb(f"x_in{p}", [128, GS, D]) for p in range(2)]
        mask_in = [sb(f"mask_in{p}", [128, GS, S], BF16) for p in range(2)]
        wsub = [sb(f"wsub{p}", [128, GS, D]) for p in range(2)]
        wi_in = [sb(f"wi_in{p}", [128, GS, F]) for p in range(2)]
        wo_in = [sb(f"wo_in{p}", [128, GS, FC, D]) for p in range(2)]
        side_in = [sb(f"side_in{p}", [128, GS, D]) for p in range(2)]
        emb_in = [sb(f"emb_in{p}", [128, GS, S]) for p in range(2)]
        x2t = [sb(f"x2t{p}", [128, GS, S]) for p in range(2)]
        x2h = [sb(f"x2h{p}", [128, N], F32R) for p in range(2)]
        x2l = [sb(f"x2l{p}", [128, N], F32R) for p in range(2)]
        out_sb = sb("out_sb", [128, B, D])
        xt = sb("xt", [128, GS, S])
        th = sb("th", [128, S])
        nmax1 = sb("nmax1", [128, GS])
        sum1 = sb("sum1", [128, GS])
        den1 = sb("den1", [128, GS])
        rec1 = sb("rec1", [128, GS])
        p1 = sb("p1", [128, GS, S])
        pn = sb("pn", [128, GS, S])
        pnt = sb("pnt", [128, GS, S])
        x1t = sb("x1t", [128, GS, S])
        h_sel = [sb(f"h_sel{i}", [128, GS, S]) for i in range(NH)]
        h_hi = [sb(f"h_hi{i}", [128, N], F32R) for i in range(NH)]
        h_lo = [sb(f"h_lo{i}", [128, N], F32R) for i in range(NH)]
        eo = sb("eo", [128, EX, GS, S])
        gprod = sb("gprod", [128, GS, EX])
        gnmax = sb("gnmax", [128, GS])
        gsh = sb("gsh", [128, GS, EX])
        gexp = sb("gexp", [128, GS, EX])
        gsum = sb("gsum", [128, GS])
        grec = sb("grec", [128, GS])
        gw = sb("gw", [128, GS, EX])
        x3t = sb("x3t", [128, GS, S])
        kt = sb("kt", [128, GS, S])
        qt = sb("qt", [128, GS, S])
        x3n = sb("x3n", [128, GS, D])
        nmax2 = sb("nmax2", [128, GS])
        sum2 = sb("sum2", [128, GS])
        rec2 = sb("rec2", [128, GS])
        p2 = sb("p2", [128, GS, S])
        p2t = sb("p2t", [128, GS, S])

        def bank(name):
            return ctx.enter_context(nc.psum_tensor(name, [128, GS, S], F32))

        fb = bank("fb")
        kb = bank("kb")
        gb = bank("gb")
        hb = [bank(f"hb{i}") for i in range(NH)]
        ab = [bank(f"ab{i}") for i in range(2)]

        ld_tok = sems("ld_tok", 3)
        ld_tokb, ld_w1, ld_rows, ld_subj, ld_bias, ld_swi, ld_swo, ld_gate = (
            sem(n) for n in ("ld_tokb", "ld_w1", "ld_rows", "ld_subj", "ld_bias", "ld_swi", "ld_swo",
                             "ld_gate"))
        ld_x, ld_mask, ld_wsub, ld_wi, ld_wo, ld_side, ld_emb = (
            sems(n) for n in ("ld_x", "ld_mask", "ld_wsub", "ld_wi", "ld_wo", "ld_side", "ld_emb"))
        st_out = sem("st_out")
        pool_set, masks_set, ident_set, tok_set, cnt_set, pads_zero, w1p_set, rows_set, cols_ps, cols_set, vp_set = (
            sem(n) for n in ("pool_set", "masks_set", "ident_set", "tok_set", "cnt_set", "pads_zero", "w1p_set",
                             "rows_set", "cols_ps", "cols_set", "vp_set"))
        onehot_set = sem("onehot_set")
        bias_ps, bias_set, subj_ps, subj_set, sw_hi, sw_lo = (
            sem(n) for n in ("bias_ps", "bias_set", "subj_ps", "subj_set", "sw_hi", "sw_lo"))
        xt_ps, xt_sb, z_ps, th_sb, sc_ps, nmax1_sb, p1_sb, den1_sb, rec1_sb, pn_sb = (
            sem(n) for n in ("xt_ps", "xt_sb", "z_ps", "th_sb", "sc_ps", "nmax1_sb", "p1_sb", "den1_sb", "rec1_sb",
                             "pn_sb"))
        pnt_ps, pnt_sb, x1_ps, x1_sb, x2_ps, x2_sb, x2h_sb, x2l_sb = (
            sem(n) for n in ("pnt_ps", "pnt_sb", "x1_ps", "x1_sb", "x2_ps", "x2_sb", "x2h_sb", "x2l_sb"))
        h_ps, h_sb, hl_sb, hid_used, eo_sb = (sem(n) for n in ("h_ps", "h_sb", "hl_sb", "hid_used", "eo_sb"))
        g1_ps, gprod_sb, g2_ps, gnmax_sb, gsh_sb, gexp_sb, gsum_sb, grec_sb, gw_sb, x3_sb = (
            sem(n) for n in ("g1_ps", "gprod_sb", "g2_ps", "gnmax_sb", "gsh_sb", "gexp_sb", "gsum_sb", "grec_sb",
                             "gw_sb", "x3_sb"))
        kt_ps, kt_sb, qt_sb, x3n_ps, x3n_sb, at_ps, nmax2_sb, p2_sb, rec2_sb, p2t_ps, p2t_sb, pv_ps, out_rdy = (
            sem(n) for n in ("kt_ps", "kt_sb", "qt_sb", "x3n_ps", "x3n_sb", "at_ps", "nmax2_sb", "p2_sb", "rec2_sb",
                             "p2t_ps", "p2t_sb", "pv_ps", "out_rdy"))

        def flat(t):
            return t[:].rearrange("p b s -> p (b s)")

        def acc_of(g, e):
            return ab[(EX * g.p + e) % 2]

        ALL = slice(0, GS)

        def one(b):
            return slice(b, b + 1)

        def count(samples):
            return samples.stop - samples.start

        def picks(eng, g, row, entries):
            return [eng.value_load(toks[0:1, row, bass.ds(g.n * GS + b, 1)], min_val=0, max_val=entries - 1)
                    for b in range(GS)]

        def front_bank(g):
            return kb if isinstance(g.n, int) and g.n == 1 else fb

        def back_bank(g, b):
            return (fb, hb[0], hb[1], hb[2])[b] if isinstance(g.n, int) and g.n == NG - 1 else kb

        def pipeline(eng, front, step, back, peeled=0):
            front(fixed(0))
            step(None, fixed(0), fixed(1))
            with eng.Fori(0, (NG - 2 - peeled) // 2) as i:
                for u in range(2):
                    step(looped(i, u), looped(i, u + 1), looped(i, u + 2))
            for g in range(NG - 1 - peeled, NG - 1):
                step(fixed(g - 1), fixed(g), fixed(g + 1))
            step(fixed(NG - 2), fixed(NG - 1), None)
            back(fixed(NG - 1))

        block = ctx.enter_context(nc.Block())

        @block.sync
        def _(sp):
            def load_x(g):
                sp.dma_start(x_in[g.p][:], x[bass.ds(g.n * GS, GS)].rearrange("b s d -> s b d")).then_inc(ld_x[g.p], 16)

            def load_mask(g, kinds):
                for b in range(GS):
                    sp.dma_start(mask_in[g.p][:, b, :], masks[:, bass.ds(kinds[b], 1), :]).then_inc(ld_mask[g.p], 16)

            def load_front(g):
                kinds = picks(sp, g, 0, NEXP)
                sp.wait_ge(x2_ps, g.n - 1)
                load_x(g)
                load_mask(g, kinds)

            def load_mid(g, kinds=None):
                kinds = kinds or picks(sp, g, 0, NEXP)
                if not g.fresh:
                    sp.wait_ge(hid_used, CH * (g.n - 2) + FC)
                for b in range(GS):
                    sp.dma_start(wi_in[g.p][:, b, :],
                                 wi[bass.ds(kinds[b], 1)].rearrange("o d f -> d (o f)")).then_inc(ld_wi[g.p], 16)
                for b in range(GS):
                    sp.dma_start(wo_in[g.p][:, b, :, :],
                                 wo[bass.ds(kinds[b], 1)].rearrange("o (c f) d -> f (o c) d", c=FC)).then_inc(ld_wo[g.p], 16)

            def load_side(g):
                if not g.fresh or not isinstance(g.n, int):
                    sp.wait_ge(h_ps, CH * g.n + 1)
                sp.dma_start(side_in[g.p][:],
                             side[bass.ds(g.n * GS, GS)].rearrange("b s d -> s b d")).then_inc(ld_side[g.p], 16)

            def store(g, b, count):
                sp.dma_start(out[bass.ds(g.n * GS + b, count)].rearrange("b s d -> s b d"),
                             out_sb[:, bass.ds(g.n * GS + b, count), :]).then_inc(st_out, 16)

            def front(g):
                for n, t in enumerate((tok_mask, tok_subj, tok_stage)):
                    sp.dma_start(toks[:, n, :], t.rearrange("(a b) -> a b", a=1)).then_inc(ld_tok[n], 16)
                    if n == 0:
                        load_x(g)
                sp.dma_start(subj_in[:], subj_w.rearrange("s o h -> o s h")).then_inc(ld_subj, 16)
                sp.wait_ge(ld_tok[0], 16)
                kinds = picks(sp, g, 0, NEXP)
                sp.wait_ge(masks_set, 3)
                load_mask(g, kinds)
                load_x(fixed(1))
                load_mid(g, kinds)
                load_mask(fixed(1), picks(sp, fixed(1), 0, NEXP))

            def step(gb_, gm, gf):
                if gf is not None:
                    load_mid(gf)
                load_side(gm)
                if gf is not None and not (isinstance(gf.n, int) and gf.n == NG - 1):
                    load_front(Group(gf.n + 1, 1 - gf.p, gf.turn + gf.p))
                if gb_ is not None:
                    sp.wait_ge(out_rdy, GS * (gb_.n + 1))
                    store(gb_, 0, GS)

            def back(g):
                for b in range(GS):
                    sp.wait_ge(out_rdy, GS * g.n + b + 1)
                    store(g, b, 1)

            pipeline(sp, front, step, back, peeled=2)
            sp.wait_ge(st_out, 16 * (NG - 1 + GS))

        @block.gpsimd
        def _(pool):
            nc.gpsimd.memset(ident[:], 0.0).then_inc(pool_set, 1)
            nc.gpsimd.memset(masks[:], 0.0).then_inc(pool_set, 1)
            nc.gpsimd.iota(row_i[:], pattern=[[0, 1]], base=0, channel_multiplier=1).then_inc(pool_set, 1)
            nc.gpsimd.memset(ones[:], 1.0).then_inc(pool_set, 1)
            pool.wait_ge(pool_set, 4)
            nc.gpsimd.affine_select(out=ident[:], in_=ident[:], compare_op=ALU.not_equal, fill=1.0, base=0,
                                    pattern=[[-1, 128]], channel_multiplier=1).then_inc(ident_set, 1)
            nc.gpsimd.affine_select(out=masks[:, 0, :], in_=masks[:, 0, :], compare_op=ALU.is_ge, fill=NEG, base=0,
                                    pattern=[[-1, S]], channel_multiplier=1).then_inc(masks_set, 1)
            nc.gpsimd.affine_select(out=masks[:, 1, :], in_=masks[:, 1, :], compare_op=ALU.is_ge, fill=NEG, base=0,
                                    pattern=[[1, S]], channel_multiplier=-1).then_inc(masks_set, 1)
            nc.gpsimd.affine_select(out=masks[:, 2:NEXP, :], in_=masks[:, 2:NEXP, :], compare_op=ALU.not_equal,
                                    fill=NEG, base=0, pattern=[[0, NEXP - 2], [-1, S]],
                                    channel_multiplier=1).then_inc(masks_set, 1)
            pool.dma_start(bias_rows[:], subj_b).then_inc(ld_bias, 16)
            pool.dma_start(swi_in[:], swi.rearrange("e d f -> d e f")).then_inc(ld_swi, 16)
            pool.dma_start(swo_in[:], swo.rearrange("e (c f) d -> f e c d", c=FC)).then_inc(ld_swo, 16)
            pool.dma_start(g1_sb[:], g1.rearrange("(c k) d -> k c d", c=EX)).then_inc(ld_gate, 16)
            pool.dma_start(g2_sb[:], g2).then_inc(ld_gate, 16)

            def load_wsub(g):
                subjs = picks(pool, g, 1, NSUB)
                for b in range(GS):
                    pool.dma_start(wsub[g.p][:, b, :], subj_t[:, bass.ds(subjs[b], 1), :]).then_inc(ld_wsub[g.p], 16)

            def load_emb(g):
                stages = picks(pool, g, 2, NSTAGE)
                for b in range(GS):
                    pool.dma_start(emb_in[g.p][:, b, :],
                                   embed[bass.ds(stages[b], 1)].to_broadcast([128, S])).then_inc(ld_emb[g.p], 16)

            def split_x2(g):
                pool.wait_ge(x2h_sb, g.n + 1)
                if not g.fresh:
                    pool.wait_ge(h_ps, CH * (g.n - 1))
                nc.gpsimd.tensor_tensor(x2l[g.p][:], flat(x2t[g.p]), x2h[g.p][:].bitcast(F32),
                                        ALU.subtract).then_inc(x2l_sb, 1)

            def query(g, samples=ALL):
                pool.wait_ge(x3_sb, EX * (GS * g.n + samples.stop))
                pool.wait_ge(ld_emb[g.p], 16 * GS * (g.turn + 1))
                nc.gpsimd.tensor_tensor(qt[:, samples, :], x3t[:, samples, :], emb_in[g.p][:, samples, :],
                                        ALU.add).then_inc(qt_sb, count(samples))

            def step(gb_, gm, gf):
                if gf is not None and not gf.fresh:
                    load_wsub(gf)
                if gb_ is not None:
                    query(gb_)
                load_emb(gm)
                if gf is not None and not gf.fresh:
                    split_x2(gf)

            def front(g):
                pool.wait_ge(ld_tok[1], 16)
                pool.wait_ge(ld_tok[2], 16)
                pool.wait_ge(subj_set, 2)
                load_wsub(g)
                load_wsub(fixed(1))
                split_x2(g)
                split_x2(fixed(1))

            def back(g):
                for b in range(GS):
                    query(g, one(b))

            pipeline(pool, front, step, back)

        @block.scalar
        def _(act):
            act.dma_start(w1_in[:], w1).then_inc(ld_w1, 16)
            for n, t in enumerate((b1, v)):
                act.dma_start(rows_in[:, n, :], t.rearrange("(o a) -> o a", o=1)).then_inc(ld_rows, 16)
            for n, t in enumerate((tok_mask, tok_subj)):
                act.dma_start(tokb[:, n, :], t.rearrange("(a b) -> a b", a=1).to_broadcast([128, B])).then_inc(ld_tokb, 16)

            def copy_xt(g):
                act.wait_ge(xt_ps, g.n + 1)
                nc.scalar.copy(flat(xt), flat(front_bank(g))).then_inc(xt_sb, 1)

            def tanh(g):
                act.wait_ge(z_ps, g.n + 1)
                nc.scalar.activation(th[:], front_bank(g)[:, 0, :], ACT.Tanh, bias=cols[:, 0:1]).then_inc(th_sb, 1)

            def exp1(g):
                act.wait_ge(nmax1_sb, g.n + 1)
                for b in range(GS):
                    nc.scalar.activation(p1[:, b, :], front_bank(g)[:, b, :], ACT.Exp, bias=nmax1[:, b:b + 1],
                                         accum_out=sum1[:, b:b + 1]).then_inc(p1_sb, 1)

            def copy_pnt(g):
                act.wait_ge(pnt_ps, g.n + 1)
                nc.scalar.copy(flat(pnt), flat(front_bank(g))).then_inc(pnt_sb, 1)

            def copy_x1(g):
                act.wait_ge(x1_ps, g.n + 1)
                nc.scalar.copy(flat(x1t), flat(front_bank(g))).then_inc(x1_sb, 1)

            def split_x2(g):
                act.wait_ge(x2_sb, g.n + 1)
                if not g.fresh:
                    act.wait_ge(h_ps, CH * (g.n - 1))
                nc.scalar.activation(x2h[g.p][:], flat(x2t[g.p]), ACT.Identity).then_inc(x2h_sb, 1)

            def hidden(g, c):
                act.wait_ge(h_ps, CH * g.n + c + 1)
                if c >= NH or not g.first:
                    act.wait_ge(hid_used, CH * g.n + c + 1 - NH)
                dst = flat(h_sel[c % NH]) if c < FC else h_hi[c % NH][:]
                nc.scalar.activation(dst, flat(hb[c % NH]), ACT.Relu).then_inc(h_sb, 1)

            def expert_out(g, e):
                act.wait_ge(hid_used, CH * g.n + FC * (e + 1))
                if not g.first:
                    act.wait_ge(x3_sb, EX * GS * g.n)
                nc.scalar.copy(eo[:, e].rearrange("p b s -> p (b s)"), flat(acc_of(g, e))).then_inc(eo_sb, 1)

            def gate(g):
                act.wait_ge(gsh_sb, g.n + 1)
                nc.scalar.activation(gexp[:], gsh[:], ACT.Exp).then_inc(gexp_sb, 1)

            def copy_kt(g):
                act.wait_ge(kt_ps, g.n + 1)
                nc.scalar.copy(flat(kt), flat(kb)).then_inc(kt_sb, 1)

            def copy_x3n(g):
                act.wait_ge(x3n_ps, GS * (g.n + 1))
                nc.scalar.copy(flat(x3n), flat(kb)).then_inc(x3n_sb, 1)

            def exp2(g, samples=ALL):
                act.wait_ge(nmax2_sb, GS * g.n + samples.stop)
                for b in range(samples.start, samples.stop):
                    nc.scalar.activation(p2[:, b, :], back_bank(g, b)[:, b, :], ACT.Exp, bias=nmax2[:, b:b + 1],
                                         accum_out=sum2[:, b:b + 1]).then_inc(p2_sb, 1)

            def copy_p2t(g, samples=ALL):
                act.wait_ge(p2t_ps, GS * g.n + samples.stop)
                nc.scalar.copy(p2t[:, samples, :], back_bank(g, samples.start)[:, samples, :]
                               ).then_inc(p2t_sb, count(samples))

            def front(g):
                h = fixed(1)
                copy_xt(g)
                act.wait_ge(cols_set, 1)
                tanh(g)
                copy_xt(h)
                exp1(g)
                tanh(h)
                copy_pnt(g)
                exp1(h)
                copy_x1(g)
                copy_pnt(h)
                split_x2(g)
                act.wait_ge(ld_swi, 16)
                nc.scalar.activation(swi_h[:], swi_in[:], ACT.Identity).then_inc(sw_hi, 1)
                copy_x1(h)
                act.wait_ge(ld_swo, 16)
                nc.scalar.activation(swo_h[:], swo_in[:], ACT.Identity).then_inc(sw_hi, 1)

            def step(gb_, gm, gf):
                for c in range(CH):
                    hidden(gm, c)
                    if c % FC == 2 and c > FC:
                        expert_out(gm, c // FC - 1)
                    if gb_ is not None:
                        if c == 2:
                            gate(gb_)
                            copy_kt(gb_)
                        if c == 5:
                            copy_x3n(gb_)
                        if c == 7:
                            exp2(gb_)
                        if c == 9:
                            copy_p2t(gb_)
                    if gf is not None and gf.fresh:
                        if c == 1:
                            split_x2(gf)
                    elif gf is not None:
                        if c == 0:
                            copy_xt(gf)
                        if c == 1:
                            tanh(gf)
                        if c == 3:
                            exp1(gf)
                        if c == 6:
                            copy_pnt(gf)
                        if c == 7:
                            copy_x1(gf)
                        if c == 9:
                            split_x2(gf)
                expert_out(gm, EX - 1)

            def back(g):
                copy_kt(g)
                gate(g)
                exp2(g, one(0))
                exp2(g, one(1))
                copy_p2t(g, one(0))
                exp2(g, one(2))
                copy_p2t(g, one(1))
                exp2(g, one(3))
                copy_x3n(g)
                copy_p2t(g, one(2))
                copy_p2t(g, one(3))

            pipeline(act, front, step, back)

        @block.vector
        def _(dve):
            def setup():
                nc.vector.memset(rows_rep[:], 0.0).then_inc(pads_zero, 1)
                nc.vector.memset(w1p[:], 0.0).then_inc(pads_zero, 1)
                nc.vector.memset(vp[:], 0.0).then_inc(pads_zero, 1)
                dve.wait_ge(ld_rows, 32)
                dve.wait_ge(pads_zero, 3)
                nc.vector.tensor_tensor(rows_rep[:], rows_rep[:],
                                        rows_in[:].rearrange("o n (u a) -> o n u a", u=1)
                                        .to_broadcast([1, 2, GS, A]), ALU.add).then_inc(rows_set, 1)
                dve.wait_ge(ld_w1, 16)
                for b in range(GS):
                    nc.vector.tensor_copy(w1p[:, b, b * A:(b + 1) * A], w1_in[:]).then_inc(w1p_set, 1)
                dve.wait_ge(cols_ps, 2)
                nc.vector.tensor_copy(cols[:], gb[:, 2, 0:2]).then_inc(cols_set, 1)
                dve.wait_ge(cols_set, 1)
                for b in range(GS):
                    rows = slice(b * A, (b + 1) * A)
                    nc.vector.tensor_scalar(vp[rows, b, :], vp[rows, b, :], cols[rows, 1:2], None,
                                            ALU.add).then_inc(vp_set, 1)
                dve.wait_ge(ident_set, 1)
                nc.vector.tensor_copy(identb[:], ident[:]).then_inc(ident_set, 1)
                dve.wait_ge(pool_set, 4)
                nc.vector.tensor_copy(row[:], row_i[:]).then_inc(tok_set, 1)
                dve.wait_ge(ld_tokb, 32)
                nc.vector.tensor_copy(tokf[:], tokb[:]).then_inc(tok_set, 1)
                dve.wait_ge(tok_set, 2)
                nc.vector.tensor_scalar(onehot[:], tokf[0:NSUB, 1, :], row[0:NSUB, 0:1], None,
                                        ALU.is_equal).then_inc(onehot_set, 1)
                nc.vector.tensor_scalar(is0[:], tokf[:, 0, :], 0.0, None, ALU.is_equal).then_inc(cnt_set, 1)
                nc.vector.tensor_scalar(is1[:], tokf[:, 0, :], 1.0, None, ALU.is_equal).then_inc(cnt_set, 1)
                nc.vector.tensor_scalar(up[:], row[:], 1.0, float(2 - S), ALU.mult, ALU.add).then_inc(cnt_set, 1)
                nc.vector.tensor_scalar(down[:], row[:], -1.0, 1.0, ALU.mult, ALU.add).then_inc(cnt_set, 1)
                dve.wait_ge(cnt_set, 4)
                nc.vector.tensor_scalar(cnt[:], is0[:], up[:, 0:1], float(S - 1), ALU.mult, ALU.add).then_inc(cnt_set, 1)
                dve.wait_ge(cnt_set, 5)
                nc.vector.scalar_tensor_tensor(out=cnt[:], in0=is1[:], scalar=down[:, 0:1], in1=cnt[:],
                                               op0=ALU.mult, op1=ALU.add).then_inc(cnt_set, 1)

            def subjects():
                for n in range(2):
                    dve.wait_ge(subj_ps, n + 1)
                    half = slice(n * NSUB // 2, (n + 1) * NSUB // 2)
                    nc.vector.tensor_tensor(subj_t[:, half, :], hb[n][:],
                                            ident[:].rearrange("p (o s) -> p o s", o=1).to_broadcast([128, GS, S]),
                                            ALU.add).then_inc(subj_set, 1)
                dve.wait_ge(bias_ps, 1)
                nc.vector.tensor_copy(bias[:], gb[:, 0, 0:B]).then_inc(bias_set, 1)

            def max1(g):
                dve.wait_ge(sc_ps, g.n + 1)
                nc.vector.tensor_reduce(nmax1[:], front_bank(g)[:], AX, ALU.max, negate=True).then_inc(nmax1_sb, 1)

            def norm1(g):
                dve.wait_ge(p1_sb, GS * (g.n + 1))
                nc.vector.tensor_tensor(den1[:], sum1[:], cnt[:, bass.ds(g.n * GS, GS)], ALU.mult).then_inc(den1_sb, 1)
                dve.wait_ge(den1_sb, g.n + 1)
                nc.vector.reciprocal(rec1[:], den1[:]).then_inc(rec1_sb, 1)
                dve.wait_ge(rec1_sb, g.n + 1)
                for b in range(GS):
                    nc.vector.scalar_tensor_tensor(out=pn[:, b, :], in0=p1[:, b, :], scalar=rec1[:, b:b + 1],
                                                   in1=ident[:], op0=ALU.mult, op1=ALU.add).then_inc(pn_sb, 1)

            def add_bias(g):
                dve.wait_ge(x2_ps, g.n + 1)
                if not g.fresh:
                    dve.wait_ge(x3_sb, EX * GS * (g.n - 1))
                nc.vector.tensor_tensor(x2t[g.p][:], front_bank(g)[:],
                                        bias[:, bass.ds(g.n * GS, GS)].rearrange("p (b o) -> p b o", o=1)
                                        .to_broadcast([128, GS, S]), ALU.add).then_inc(x2_sb, 1)

            def hidden_low(g, c):
                dve.wait_ge(h_sb, CH * g.n + c + 1)
                nc.vector.scalar_tensor_tensor(out=h_lo[c % NH][:], in0=flat(hb[c % NH]), scalar=0.0,
                                               in1=h_hi[c % NH][:].bitcast(F32), op0=ALU.max,
                                               op1=ALU.subtract).then_inc(hl_sb, 1)

            def gate1(g):
                dve.wait_ge(g1_ps, g.n + 1)
                nc.vector.scalar_tensor_tensor(
                    out=gprod[:], in0=gb[:, 0, 0:GS].rearrange("p (b o) -> p b o", o=1).to_broadcast([128, GS, EX]),
                    scalar=0.0, in1=g2_sb[:].rearrange("p (o e) -> p o e", o=1).to_broadcast([128, GS, EX]),
                    op0=ALU.max, op1=ALU.mult).then_inc(gprod_sb, 1)

            def gate2(g):
                dve.wait_ge(g2_ps, g.n + 1)
                logits = gb[:, 1, 0:GS * EX].rearrange("p (b e) -> p b e", e=EX)
                nc.vector.tensor_reduce(gnmax[:], logits, AX, ALU.max, negate=True).then_inc(gnmax_sb, 1)
                dve.wait_ge(gnmax_sb, g.n + 1)
                nc.vector.tensor_tensor(gsh[:], logits, gnmax[:].rearrange("p (b o) -> p b o", o=1)
                                        .to_broadcast([128, GS, EX]), ALU.add).then_inc(gsh_sb, 1)

            def gate3(g, mixed=True):
                dve.wait_ge(gexp_sb, g.n + 1)
                nc.vector.tensor_reduce(gsum[:], gexp[:], AX, ALU.add).then_inc(gsum_sb, 1)
                dve.wait_ge(gsum_sb, g.n + 1)
                nc.vector.reciprocal(grec[:], gsum[:]).then_inc(grec_sb, 1)
                dve.wait_ge(grec_sb, g.n + 1)
                nc.vector.tensor_tensor(gw[:], gexp[:], grec[:].rearrange("p (b o) -> p b o", o=1)
                                        .to_broadcast([128, GS, EX]), ALU.mult).then_inc(gw_sb, 1)
                dve.wait_ge(gw_sb, g.n + 1)
                if not mixed:
                    return
                for e in range(EX):
                    for b in range(GS):
                        mix(g, b, e, EX * GS * g.n + GS * (e - 1) + b + 1)

            def mix(g, b, e, before):
                if e:
                    dve.wait_ge(x3_sb, before)
                nc.vector.scalar_tensor_tensor(out=x3t[:, b, :], in0=eo[:, e, b, :], scalar=gw[:, b, e:e + 1],
                                               in1=(x3t if e else x2t[g.p])[:, b, :], op0=ALU.mult,
                                               op1=ALU.add).then_inc(x3_sb, 1)

            def max2(g, samples=ALL):
                dve.wait_ge(at_ps, GS * g.n + samples.stop)
                nc.vector.tensor_reduce(nmax2[:, samples], back_bank(g, samples.start)[:, samples, :], AX, ALU.max,
                                        negate=True).then_inc(nmax2_sb, count(samples))

            def norm2(g, samples=ALL):
                dve.wait_ge(p2_sb, GS * g.n + samples.stop)
                nc.vector.reciprocal(rec2[:, samples], sum2[:, samples]).then_inc(rec2_sb, count(samples))

            def result(g, samples=ALL):
                dve.wait_ge(pv_ps, GS * g.n + samples.stop)
                dve.wait_ge(x3n_sb, g.n + 1)
                dve.wait_ge(rec2_sb, GS * g.n + samples.stop)
                for b in range(samples.start, samples.stop):
                    nc.vector.scalar_tensor_tensor(out=out_sb[:, bass.ds(g.n * GS + b, 1), :],
                                                   in0=back_bank(g, b)[:, b, :], scalar=rec2[:, b:b + 1],
                                                   in1=x3n[:, b, :], op0=ALU.mult, op1=ALU.add).then_inc(out_rdy, 1)

            def front(g):
                h = fixed(1)
                setup()
                max1(g)
                norm1(g)
                subjects()
                max1(h)
                norm1(h)
                add_bias(g)
                dve.wait_ge(sw_hi, 1)
                nc.vector.tensor_tensor(swi_l[:], swi_in[:], swi_h[:].bitcast(F32), ALU.subtract).then_inc(sw_lo, 1)
                add_bias(h)
                dve.wait_ge(sw_hi, 2)
                nc.vector.tensor_tensor(swo_l[:], swo_in[:], swo_h[:].bitcast(F32), ALU.subtract).then_inc(sw_lo, 1)

            def step(gb_, gm, gf):
                for c in range(CH):
                    if c >= FC:
                        hidden_low(gm, c)
                    if gb_ is not None:
                        if c == 1:
                            gate1(gb_)
                        if c == 2:
                            gate2(gb_)
                    if gf is not None and not gf.fresh:
                        if c == 2:
                            max1(gf)
                        if c == 4:
                            norm1(gf)
                        if c == 8:
                            add_bias(gf)
                    if gb_ is not None:
                        if c == 2:
                            gate3(gb_)
                        if c == 6:
                            max2(gb_)
                        if c == 8:
                            norm2(gb_)
                if gb_ is not None:
                    result(gb_)

            def back(g):
                def shares(b):
                    for e in range(EX):
                        mix(g, b, e, EX * (GS * g.n + b) + e)

                gate1(g)
                gate2(g)
                gate3(g, mixed=False)
                shares(0)
                shares(1)
                max2(g, one(0))
                shares(2)
                max2(g, one(1))
                shares(3)
                norm2(g, one(0))
                max2(g, one(2))
                norm2(g, one(1))
                max2(g, one(3))
                result(g, one(0))
                norm2(g, one(2))
                result(g, one(1))
                norm2(g, one(3))
                result(g, one(2))
                result(g, one(3))

            pipeline(dve, front, step, back)

        @block.tensor
        def _(pe):
            def columns():
                pe.wait_ge(rows_set, 1)
                pe.wait_ge(pool_set, 4)
                for n in range(2):
                    nc.tensor.matmul(gb[:, 2, n:n + 1], rows_rep[:, n].rearrange("o b a -> o (b a)"), ones[0:1, 0:1],
                                     start=True, stop=True).then_inc(cols_ps, 1)

            def subjects():
                pe.wait_ge(ld_subj, 16)
                for n in range(NSUB):
                    t = nc.tensor.transpose(hb[n // GS][:, n % GS, :], subj_in[:, n, :], ident[:])
                    if n % GS == GS - 1:
                        t.then_inc(subj_ps, 1)
                pe.wait_ge(onehot_set, 1)
                pe.wait_ge(ld_bias, 16)
                pe.wait_ge(cols_set, 1)
                nc.tensor.matmul(gb[:, 0, 0:B], bias_rows[:], onehot[:], start=True, stop=True).then_inc(bias_ps, 1)

            def x_turn(g):
                pe.wait_ge(ld_x[g.p], 16 * (g.turn + 1))
                if not g.fresh:
                    pe.wait_ge(x2_sb, g.n)
                for b in range(GS):
                    t = nc.tensor.transpose(front_bank(g)[:, b, :], x_in[g.p][:, b, :], ident[:])
                t.then_inc(xt_ps, 1)

            def z(g):
                pe.wait_ge(xt_sb, g.n + 1)
                for b in range(GS):
                    m = nc.tensor.matmul(front_bank(g)[:, 0, :], w1p[:, b, :], xt[:, b, :], start=b == 0, stop=b == GS - 1)
                m.then_inc(z_ps, 1)

            def scores1(g):
                pe.wait_ge(th_sb, g.n + 1)
                pe.wait_ge(ld_mask[g.p], 16 * GS * (g.turn + 1))
                for b in range(GS):
                    nc.tensor.matmul(front_bank(g)[:, b, :], identb[:], mask_in[g.p][:, b, :], start=True, stop=False)
                    m = nc.tensor.matmul(front_bank(g)[:, b, :], vp[:, b, :], th[:], start=False, stop=True)
                m.then_inc(sc_ps, 1)

            def pn_turn(g):
                pe.wait_ge(pn_sb, GS * (g.n + 1))
                for b in range(GS):
                    t = nc.tensor.transpose(front_bank(g)[:, b, :], pn[:, b, :], ident[:])
                t.then_inc(pnt_ps, 1)

            def pooled(g):
                pe.wait_ge(pnt_sb, g.n + 1)
                for b in range(GS):
                    m = nc.tensor.matmul(front_bank(g)[:, b, :], x_in[g.p][:, b, :], pnt[:, b, :], start=True, stop=True)
                m.then_inc(x1_ps, 1)

            def subject(g):
                pe.wait_ge(x1_sb, g.n + 1)
                pe.wait_ge(ld_wsub[g.p], 16 * GS * (g.turn + 1))
                for b in range(GS):
                    m = nc.tensor.matmul(front_bank(g)[:, b, :], wsub[g.p][:, b, :], x1t[:, b, :], start=True, stop=True)
                m.then_inc(x2_ps, 1)

            def hid(g, c):
                e, k = c // FC, c % FC
                cols = slice(k * 128, (k + 1) * 128)
                dst = hb[c % NH]
                if c >= NH or not g.first:
                    pe.wait_ge(h_sb, CH * g.n + c + 1 - NH)
                    if c >= NH + FC:
                        pe.wait_ge(hl_sb, (CH - FC) * g.n + c + 1 - NH - FC)
                    elif c < NH:
                        pe.wait_ge(hl_sb, (CH - FC) * g.n + c + 1 - NH)
                if e == 0:
                    if k == 0:
                        pe.wait_ge(x2_sb, g.n + 1)
                        pe.wait_ge(ld_wi[g.p], 16 * GS * (g.turn + 1))
                    for b in range(GS):
                        m = nc.tensor.matmul(dst[:, b, :], wi_in[g.p][:, b, cols], x2t[g.p][:, b, :],
                                             start=True, stop=True)
                else:
                    if e == 1 and k == 0:
                        pe.wait_ge(x2l_sb, g.n + 1)
                        if g.first:
                            pe.wait_ge(sw_lo, 1)
                    nc.tensor.matmul(flat(dst), swi_h[:, e - 1, cols], x2h[g.p][:], start=True, stop=False)
                    nc.tensor.matmul(flat(dst), swi_h[:, e - 1, cols], x2l[g.p][:], start=False, stop=False)
                    m = nc.tensor.matmul(flat(dst), swi_l[:, e - 1, cols], x2h[g.p][:], start=False, stop=True)
                m.then_inc(h_ps, 1)

            def outp(g, c):
                e, k = c // FC, c % FC
                acc = acc_of(g, e)
                if k == 0 and (e >= 2 or not g.first):
                    pe.wait_ge(eo_sb, EX * g.n + e - 1)
                if e == 0:
                    pe.wait_ge(h_sb, CH * g.n + c + 1)
                    if k == 0:
                        pe.wait_ge(ld_wo[g.p], 16 * GS * (g.turn + 1))
                    for b in range(GS):
                        m = nc.tensor.matmul(acc[:, b, :], wo_in[g.p][:, b, k, :], h_sel[c % NH][:, b, :],
                                             start=k == 0 and b == 0, stop=k == FC - 1, skip_group_check=True)
                else:
                    if e == 1 and k == 0 and g.first:
                        pe.wait_ge(sw_lo, 2)
                    pe.wait_ge(hl_sb, (CH - FC) * g.n + c + 1 - FC)
                    hh, hl = h_hi[c % NH][:], h_lo[c % NH][:]
                    nc.tensor.matmul(flat(acc), swo_h[:, e - 1, k, :], hh, start=k == 0, stop=False)
                    nc.tensor.matmul(flat(acc), swo_l[:, e - 1, k, :], hh, start=False, stop=False)
                    m = nc.tensor.matmul(flat(acc), swo_h[:, e - 1, k, :], hl, start=False, stop=k == FC - 1)
                m.then_inc(hid_used, 1)

            def gate1(g):
                pe.wait_ge(eo_sb, EX * (g.n + 1))
                for e in range(EX):
                    m = nc.tensor.matmul(gb[:, 0, 0:GS], g1_sb[:, e, :], eo[:, e, :, 0], start=e == 0, stop=e == EX - 1)
                m.then_inc(g1_ps, 1)

            def gate2(g):
                pe.wait_ge(gprod_sb, g.n + 1)
                nc.tensor.matmul(gb[:, 1, 0:GS * EX], ones[:], gprod[:].rearrange("p b e -> p (b e)"),
                                 start=True, stop=True).then_inc(g2_ps, 1)

            def key_turn(g):
                pe.wait_ge(ld_side[g.p], 16 * (g.turn + 1))
                for b in range(GS):
                    t = nc.tensor.transpose(kb[:, b, :], side_in[g.p][:, b, :], ident[:])
                t.then_inc(kt_ps, 1)

            def x3_turn(g, samples=ALL):
                pe.wait_ge(x3_sb, EX * (GS * g.n + samples.stop))
                pe.wait_ge(kt_sb, g.n + 1)
                for b in range(samples.start, samples.stop):
                    t = nc.tensor.transpose(kb[:, b, :], x3t[:, b, :], ident[:])
                t.then_inc(x3n_ps, count(samples))

            def scores2(g, samples=ALL):
                pe.wait_ge(qt_sb, GS * g.n + samples.stop)
                if back_bank(g, 0) is kb:
                    pe.wait_ge(x3n_sb, g.n + 1)
                for b in range(samples.start, samples.stop):
                    m = nc.tensor.matmul(back_bank(g, b)[:, b, :], qt[:, b, :], kt[:, b, :], start=True, stop=True)
                m.then_inc(at_ps, count(samples))

            def p2_turn(g, samples=ALL):
                pe.wait_ge(p2_sb, GS * g.n + samples.stop)
                for b in range(samples.start, samples.stop):
                    t = nc.tensor.transpose(back_bank(g, b)[:, b, :], p2[:, b, :], ident[:])
                t.then_inc(p2t_ps, count(samples))

            def attend(g, samples=ALL):
                pe.wait_ge(p2t_sb, GS * g.n + samples.stop)
                for b in range(samples.start, samples.stop):
                    m = nc.tensor.matmul(back_bank(g, b)[:, b, :], p2t[:, b, :], side_in[g.p][:, b, :],
                                         start=True, stop=True)
                m.then_inc(pv_ps, count(samples))

            def front(g):
                h = fixed(1)
                pe.wait_ge(ident_set, 1)
                x_turn(g)
                columns()
                pe.wait_ge(w1p_set, GS)
                z(g)
                x_turn(h)
                pe.wait_ge(vp_set, GS)
                pe.wait_ge(ident_set, 2)
                scores1(g)
                subjects()
                z(h)
                pn_turn(g)
                scores1(h)
                pooled(g)
                pn_turn(h)
                pe.wait_ge(bias_set, 1)
                subject(g)
                pooled(h)
                pe.wait_ge(subj_set, 2)
                pe.wait_ge(ld_gate, 32)

            def step(gb_, gm, gf):
                for c in range(CH + 2):
                    if c == CH and gb_ is not None:
                        attend(gb_)
                    if c < CH:
                        hid(gm, c)
                    if c >= 2:
                        outp(gm, c - 2)
                    if gb_ is not None:
                        if c == 1:
                            gate1(gb_)
                        if c == 2:
                            gate2(gb_)
                            key_turn(gb_)
                        if c == 5:
                            x3_turn(gb_)
                        if c == 6:
                            scores2(gb_)
                        if c == 8:
                            p2_turn(gb_)
                    if gf is not None and gf.fresh:
                        if c == 0:
                            subject(gf)
                    elif gf is not None:
                        if c == 0:
                            x_turn(gf)
                        if c == 1:
                            z(gf)
                        if c == 2:
                            scores1(gf)
                        if c == 6:
                            pn_turn(gf)
                        if c == 7:
                            pooled(gf)
                        if c == 8:
                            subject(gf)

            def back(g):
                pe.wait_ge(out_rdy, GS * g.n)
                key_turn(g)
                gate1(g)
                gate2(g)
                for b in range(GS + 2):
                    if b < GS:
                        x3_turn(g, one(b))
                        scores2(g, one(b))
                    if b >= 2:
                        p2_turn(g, one(b - 2))
                        attend(g, one(b - 2))

            pipeline(pe, front, step, back)


_INS = ["x", "itok_B_0_2", "itok_B_0_7", "fside_BxSxS_0", "itok_B_0_5", "L0_cond_W1", "L0_cond_b1", "L0_cond_v",
        "L1_cond_weight", "L1_cond_bias", "L2_cond_wi", "L2_cond_wo", "L2_cond_swi", "L2_cond_swo", "L2_cond_g1",
        "L2_cond_g2", "L3_cond_braak_embed"]


def kernel(**inputs):
    import concourse.bacc as bacc
    import numpy as np
    from concourse.bass_utils import run_bass_kernel_spmd

    nc = bacc.Bacc("TRN2", target_bir_lowering=False, num_devices=1)
    arrays, args = {}, []
    for name in _INS:
        a = np.ascontiguousarray(inputs[name])
        arrays[f"in_{name}"] = a
        args.append(nc.dram_tensor(f"in_{name}", a.shape, mybir.dt.from_np(a.dtype), kind="ExternalInput").ap())
    out = nc.dram_tensor("out", inputs["x"].shape, F32, kind="ExternalOutput").ap()
    build(nc, *args, out)
    return run_bass_kernel_spmd(nc, [arrays], core_ids=[0]).results[0]["out"]
```

```python
from contextlib import ExitStack

import concourse.bass as bass
from concourse import mybir

F32 = mybir.dt.float32
F32R = mybir.dt.float32r
BF16 = mybir.dt.bfloat16
I32 = mybir.dt.int32
ALU = mybir.AluOpType
ACT = mybir.ActivationFunctionType
AX = mybir.AxisListType.X

GS = 4
NEG = -1e30


class Group:

    def __init__(self, number, slot, turn):
        self.n, self.p, self.turn = number, slot, turn
        self.first = isinstance(number, int) and number == 0
        self.fresh = isinstance(turn, int) and turn == 0


def fixed(n):
    return Group(n, n % 2, n // 2)


def looped(i, off):
    return Group(i * 2 + off, off % 2, i + off // 2)


def build(nc, x, tok_mask, tok_subj, side, tok_stage, w1, b1, v, subj_w, subj_b, wi, wo, swi, swo, g1, g2, embed, out):
    B, S, D = x.shape
    A = w1.shape[1]
    NSUB = subj_w.shape[0]
    NEXP, _, F = wi.shape
    NSTAGE = embed.shape[0]
    NSH = swi.shape[0]
    FC = F // 128
    NG = B // GS
    EX = 1 + NSH
    CH = EX * FC
    NH = 4
    LAG = 3
    N = GS * S
    assert NSUB == 2 * GS and S == 128 and D == 128 and GS * A == 128 and NG % 2 == 0 and N == 512

    with ExitStack() as ctx:
        def sb(name, shape, dt=F32):
            return ctx.enter_context(nc.sbuf_tensor(name, shape, dt))

        def sem(name):
            return ctx.enter_context(nc.semaphore(name))

        def sems(name, n=2):
            return [sem(f"{name}{i}") for i in range(n)]

        ident = sb("ident", [128, 128])
        identb = sb("identb", [128, 128], BF16)
        ones = sb("ones", [128, 128])
        side_of = sb("side_of", [128, S], BF16)
        toks = sb("toks", [1, 3, B], I32)
        tokb = sb("tokb", [128, 2, B], I32)
        tokf = sb("tokf", [128, 2, B])
        row_i = sb("row_i", [128, 1], I32)
        row = sb("row", [128, 1])
        kind = sb("kind", [128, B])
        is0 = sb("is0", [128, B])
        is1 = sb("is1", [128, B])
        up = sb("up", [128, 1])
        down = sb("down", [128, 1])
        cnt = sb("cnt", [128, B])
        onehot = sb("onehot", [NSUB, B])
        bias_rows = sb("bias_rows", [NSUB, D])
        bias = sb("bias", [128, B])
        w1_in = sb("w1_in", [128, A])
        rows_in = sb("rows_in", [1, 2, A])
        rows_rep = sb("rows_rep", [1, 2, GS, A])
        cols = sb("cols", [128, 2])
        w1_h = sb("w1_h", [128, GS, A], F32R)
        w1_l = sb("w1_l", [128, GS, A], F32R)
        zeros = sb("zeros", [128, N], BF16)
        spare = sb("spare", [128, 1])
        started = sb("started", [128, 1])
        is_lo = sb("is_lo", [128, 1])
        v_h = sb("v_h", [128, 1], F32R)
        v_neg = sb("v_neg", [128, 1])
        vs = sb("vs", [128, 128], F32R)
        subj_in = sb("subj_in", [128, NSUB, D])
        subj_t = sb("subj_t", [128, NSUB, D])
        swi_in = sb("swi_in", [128, NSH, F])
        swi_h = sb("swi_h", [128, NSH, F], F32R)
        swi_l = sb("swi_l", [128, NSH, F], F32R)
        swo_in = sb("swo_in", [128, NSH, FC, D])
        swo_h = sb("swo_h", [128, NSH, FC, D], F32R)
        swo_l = sb("swo_l", [128, NSH, FC, D], F32R)
        g1_sb = sb("g1_sb", [128, EX, D])
        g2_sb = sb("g2_sb", [128, EX])

        x_in = [sb(f"x_in{p}", [128, GS, D]) for p in range(2)]
        wsub = [sb(f"wsub{p}", [128, GS, D]) for p in range(2)]
        wi_in = [sb(f"wi_in{p}", [128, GS, F]) for p in range(2)]
        wo_in = [sb(f"wo_in{p}", [128, GS, FC, D]) for p in range(2)]
        side_in = [sb(f"side_in{p}", [128, GS, D]) for p in range(2)]
        emb_in = [sb(f"emb_in{p}", [128, GS, S]) for p in range(2)]
        x2t = [sb(f"x2t{p}", [128, GS, S]) for p in range(2)]
        x2h = [sb(f"x2h{p}", [128, N], F32R) for p in range(2)]
        x2l = [sb(f"x2l{p}", [128, N], F32R) for p in range(2)]
        out_sb = sb("out_sb", [128, B, D])
        mask = sb("mask", [128, GS, S], BF16)
        xt_h = sb("xt_h", [128, GS, S], F32R)
        xt_l = sb("xt_l", [128, GS, S], F32R)
        th = sb("th", [128, GS, S])
        ths = sb("ths", [128, GS, S], F32R)
        nmax1 = sb("nmax1", [128, GS])
        sum1 = sb("sum1", [128, GS])
        den1 = sb("den1", [128, GS])
        rec1 = sb("rec1", [128, GS])
        p1 = sb("p1", [128, GS, S])
        pn = sb("pn", [128, GS, S])
        pnt = sb("pnt", [128, GS, S])
        x1t = sb("x1t", [128, GS, S])
        h_sel = [sb(f"h_sel{i}", [128, GS, S]) for i in range(NH)]
        h_hi = [sb(f"h_hi{i}", [128, N], F32R) for i in range(NH)]
        h_lo = [sb(f"h_lo{i}", [128, N], F32R) for i in range(NH)]
        eo = sb("eo", [128, EX, GS, S])
        gprod = sb("gprod", [128, GS, EX])
        gnmax = sb("gnmax", [128, GS])
        gsh = sb("gsh", [128, GS, EX])
        gexp = sb("gexp", [128, GS, EX])
        gsum = sb("gsum", [128, GS])
        grec = sb("grec", [128, GS])
        gw = sb("gw", [128, GS, EX])
        x3t = sb("x3t", [128, GS, S])
        kt = sb("kt", [128, GS, S])
        qt = sb("qt", [128, GS, S])
        x3n = sb("x3n", [128, GS, D])
        nmax2 = sb("nmax2", [128, GS])
        sum2 = sb("sum2", [128, GS])
        rec2 = sb("rec2", [128, GS])
        p2 = sb("p2", [128, GS, S])
        p2t = sb("p2t", [128, GS, S])

        def bank(name):
            return ctx.enter_context(nc.psum_tensor(name, [128, GS, S], F32))

        fb = bank("fb")
        kb = bank("kb")
        hb = [bank(f"hb{i}") for i in range(NH)]
        ab = [bank(f"ab{i}") for i in range(2)]

        ld_tok = sems("ld_tok", 3)
        ld_tokb, ld_w1, ld_rows, ld_subj, ld_bias, ld_swi, ld_swo, ld_gate = (
            sem(n) for n in ("ld_tokb", "ld_w1", "ld_rows", "ld_subj", "ld_bias", "ld_swi", "ld_swo",
                             "ld_gate"))
        ld_x, ld_wsub, ld_wi, ld_wo, ld_side, ld_emb = (
            sems(n) for n in ("ld_x", "ld_wsub", "ld_wi", "ld_wo", "ld_side", "ld_emb"))
        ld_wsub0 = sems("ld_wsub0")
        ld_wsub_last = sem("ld_wsub_last")
        st_out = sem("st_out")
        pool_set, sides_set, ident_set, tok_set, cnt_set, rep_zero, w1_set, rows_set, cols_ps, cols_set, vs_set = (
            sem(n) for n in ("pool_set", "sides_set", "ident_set", "tok_set", "cnt_set", "rep_zero", "w1_set",
                             "rows_set", "cols_ps", "cols_set", "vs_set"))
        onehot_set, spare_set, kind_set, subj_in_set, subj_in2_set, lo_set, mask_sb, share0_01_sb, share0_23_sb, token0_sb = (
            sem(n) for n in ("onehot_set", "spare_set", "kind_set", "subj_in_set", "subj_in2_set", "lo_set",
                             "mask_sb", "share0_01_sb", "share0_23_sb", "token0_sb"))
        bias_ps, bias_set, subj_ps, subj_set, sw_hi, sw_lo = (
            sem(n) for n in ("bias_ps", "bias_set", "subj_ps", "subj_set", "sw_hi", "sw_lo"))
        xt_ps, xth_sb, xtl_sb, z_ps, th_sb, ths_sb, sc_ps, nmax1_sb, p1_sb, den1_sb, rec1_sb, pn_sb = (
            sem(n) for n in ("xt_ps", "xth_sb", "xtl_sb", "z_ps", "th_sb", "ths_sb", "sc_ps", "nmax1_sb", "p1_sb",
                             "den1_sb", "rec1_sb", "pn_sb"))
        pnt_ps, pnt_sb, x1_ps, x1_sb, x2_ps, x2_sb, x2h_sb, x2l_sb = (
            sem(n) for n in ("pnt_ps", "pnt_sb", "x1_ps", "x1_sb", "x2_ps", "x2_sb", "x2h_sb", "x2l_sb"))
        h_ps, h_sb, hl_sb, hid_used, eo_sb = (sem(n) for n in ("h_ps", "h_sb", "hl_sb", "hid_used", "eo_sb"))
        g1_ps, gprod_sb, g2_ps, gnmax_sb, gsh_sb, gexp_sb, gsum_sb, grec_sb, gw_sb, x3_sb = (
            sem(n) for n in ("g1_ps", "gprod_sb", "g2_ps", "gnmax_sb", "gsh_sb", "gexp_sb", "gsum_sb", "grec_sb",
                             "gw_sb", "x3_sb"))
        kt_ps, kt_sb, qt_sb, x3n_ps, x3n_sb, at_ps, nmax2_sb, p2_sb, rec2_sb, p2t_ps, p2t_sb, pv_ps, out_rdy = (
            sem(n) for n in ("kt_ps", "kt_sb", "qt_sb", "x3n_ps", "x3n_sb", "at_ps", "nmax2_sb", "p2_sb", "rec2_sb",
                             "p2t_ps", "p2t_sb", "pv_ps", "out_rdy"))

        def flat(t, samples=slice(0, GS)):
            return t[:, samples, :].rearrange("p b s -> p (b s)")

        def acc_of(g, e):
            return ab[(EX * g.p + e) % 2]

        ident_wide = ident[:].rearrange("p (o s) -> p o s", o=1).to_broadcast([128, GS, S])
        ALL = slice(0, GS)
        HALVES = (slice(0, GS // 2), slice(GS // 2, GS))

        def one(b):
            return slice(b, b + 1)

        def count(samples):
            return samples.stop - samples.start

        def picks(eng, g, row, entries, samples=ALL):
            return [eng.value_load(toks[0:1, row, bass.ds(g.n * GS + b, 1)], min_val=0, max_val=entries - 1)
                    for b in range(samples.start, samples.stop)]

        def front_bank(g, samples=ALL):
            if g.first:
                return fb if samples.start == 0 else ab[1]
            return kb if isinstance(g.n, int) and g.n == 1 else fb

        def back_bank(g, b):
            return (fb, hb[0], hb[1], hb[2])[b] if isinstance(g.n, int) and g.n == NG - 1 else kb

        def key_bank(g):
            return acc_of(g, 1) if isinstance(g.n, int) and g.n == NG - 1 else kb

        def tail_mixed(g, b, e):
            return EX * GS * g.n + (EX - 1) * (b - b % 2) + 2 * (e - 1) + b % 2 + 1

        def pipeline(eng, front, step, back, peeled=0):
            front(fixed(0))
            step(None, fixed(0), fixed(1))
            with eng.Fori(0, (NG - 2 - peeled) // 2) as i:
                for u in range(2):
                    step(looped(i, u), looped(i, u + 1), looped(i, u + 2))
            for g in range(NG - 1 - peeled, NG - 1):
                step(fixed(g - 1), fixed(g), fixed(g + 1))
            step(fixed(NG - 2), fixed(NG - 1), None)
            back(fixed(NG - 1))

        block = ctx.enter_context(nc.Block())

        @block.sync
        def _(sp):
            def load_x(g):
                sp.dma_start(x_in[g.p][:],
                             x[bass.ds(g.n * GS, GS)].rearrange("b s d -> s b d")).then_inc(ld_x[g.p], 16)

            def load_front(g):
                if not g.fresh:
                    sp.wait_ge(x2_ps, GS * (g.n - 1))
                load_x(g)

            def load_mid(g):
                kinds = picks(sp, g, 0, NEXP)
                if g.first:
                    sp.wait_ge(ld_tok[1], 16)
                    subj = picks(sp, g, 1, NSUB, one(GS - 1))[0]
                if not g.fresh:
                    sp.wait_ge(hid_used, CH * (g.n - 2) + FC)
                if g.first:
                    sp.wait_ge(subj_set, 2)
                    sp.dma_start(wsub[g.p][:, GS - 1, :], subj_t[:, bass.ds(subj, 1), :]).then_inc(ld_wsub_last, 16)
                for b in range(GS):
                    sp.dma_start(wi_in[g.p][:, b, :],
                                 wi[bass.ds(kinds[b], 1)].rearrange("o d f -> d (o f)")).then_inc(ld_wi[g.p], 16)
                for b in range(GS):
                    sp.dma_start(wo_in[g.p][:, b, :, :],
                                 wo[bass.ds(kinds[b], 1)].rearrange("o (c f) d -> f (o c) d", c=FC)).then_inc(ld_wo[g.p], 16)

            def load_side(g):
                if not g.fresh or not isinstance(g.n, int):
                    sp.wait_ge(h_ps, CH * g.n + 1)
                sp.dma_start(side_in[g.p][:],
                             side[bass.ds(g.n * GS, GS)].rearrange("b s d -> s b d")).then_inc(ld_side[g.p], 16)

            def store(g, b, count):
                sp.dma_start(out[bass.ds(g.n * GS + b, count)].rearrange("b s d -> s b d"),
                             out_sb[:, bass.ds(g.n * GS + b, count), :]).then_inc(st_out, 16)

            def front(g):
                def token_row(n):
                    t = (tok_mask, tok_subj, tok_stage)[n]
                    sp.dma_start(toks[:, n, :], t.rearrange("(a b) -> a b", a=1)).then_inc(ld_tok[n], 16)

                load_x(g)
                for n, t in enumerate((b1, v)):
                    sp.dma_start(rows_in[:, n, :], t.rearrange("(o a) -> o a", o=1)).then_inc(ld_rows, 16)
                sp.dma_start(w1_in[:], w1).then_inc(ld_w1, 16)
                for n, t in enumerate((tok_mask, tok_subj)):
                    sp.dma_start(tokb[:, n, :],
                                 t.rearrange("(a b) -> a b", a=1).to_broadcast([128, B])).then_inc(ld_tokb, 16)
                sp.dma_start(subj_in[:], subj_w.rearrange("s o h -> o s h")).then_inc(ld_subj, 16)
                token_row(1)
                token_row(0)
                load_x(fixed(1))
                sp.dma_start(bias_rows[:], subj_b).then_inc(ld_bias, 16)
                token_row(2)
                sp.dma_start(swi_in[:], swi.rearrange("e d f -> d e f")).then_inc(ld_swi, 16)
                sp.dma_start(swo_in[:], swo.rearrange("e (c f) d -> f e c d", c=FC)).then_inc(ld_swo, 16)
                sp.wait_ge(ld_tok[0], 16)
                load_mid(g)
                sp.dma_start(g1_sb[:], g1.rearrange("(c k) d -> k c d", c=EX)).then_inc(ld_gate, 16)
                sp.dma_start(g2_sb[:], g2).then_inc(ld_gate, 16)

            def step(gb_, gm, gf):
                if gf is not None:
                    load_mid(gf)
                load_side(gm)
                if gf is not None and not (isinstance(gf.n, int) and gf.n == NG - 1):
                    load_front(Group(gf.n + 1, 1 - gf.p, gf.turn + gf.p))
                if gb_ is not None:
                    sp.wait_ge(out_rdy, GS * (gb_.n + 2))
                    store(gb_, 0, GS)

            def back(g):
                for b in (h.start for h in HALVES):
                    sp.wait_ge(out_rdy, GS * (g.n + 1) + b + 2)
                    store(g, b, 2)

            pipeline(sp, front, step, back, peeled=2)
            sp.wait_ge(st_out, 16 * (NG - 1 + len(HALVES)))

        @block.gpsimd
        def _(pool):
            nc.gpsimd.memset(ident[:], 0.0).then_inc(pool_set, 1)
            nc.gpsimd.memset(zeros[:], 0.0).then_inc(pool_set, 1)
            nc.gpsimd.iota(row_i[:], pattern=[[0, 1]], base=0, channel_multiplier=1).then_inc(pool_set, 1)
            nc.gpsimd.memset(ones[:], 1.0).then_inc(pool_set, 1)
            nc.gpsimd.memset(side_of[:], 2.0).then_inc(pool_set, 1)
            pool.wait_ge(pool_set, 5)
            nc.gpsimd.affine_select(out=ident[:], in_=ident[:], compare_op=ALU.not_equal, fill=1.0, base=0,
                                    pattern=[[-1, 128]], channel_multiplier=1).then_inc(ident_set, 1)
            nc.gpsimd.affine_select(out=side_of[:], in_=side_of[:], compare_op=ALU.is_ge, fill=0.0, base=0,
                                    pattern=[[-1, S]], channel_multiplier=1).then_inc(sides_set, 1)
            pool.wait_ge(sides_set, 1)
            nc.gpsimd.affine_select(out=side_of[:], in_=side_of[:], compare_op=ALU.is_ge, fill=1.0, base=0,
                                    pattern=[[1, S]], channel_multiplier=-1).then_inc(sides_set, 1)

            def add_residual():
                pool.wait_ge(ld_subj, 16)
                pool.wait_ge(ident_set, 1)
                nc.gpsimd.tensor_tensor(subj_in[:, GS:, :], subj_in[:, GS:, :], ident_wide,
                                        ALU.add).then_inc(subj_in2_set, 1)

            def load_wsub(g):
                samples = slice(0, GS - 1) if g.first else ALL
                subjs = picks(pool, g, 1, NSUB, samples)
                if g.first:
                    pool.wait_ge(subj_set, 2)
                for b in range(count(samples)):
                    pool.dma_start(wsub[g.p][:, b, :], subj_t[:, bass.ds(subjs[b], 1), :]
                                   ).then_inc(ld_wsub0[b * 2 // GS] if g.first else ld_wsub[g.p], 16)

            def load_emb(g):
                stages = picks(pool, g, 2, NSTAGE)
                for b in range(GS):
                    pool.dma_start(emb_in[g.p][:, b, :],
                                   embed[bass.ds(stages[b], 1)].to_broadcast([128, S])).then_inc(ld_emb[g.p], 16)

            def split_x2(g):
                pool.wait_ge(x2h_sb, g.n + 1)
                if not g.fresh:
                    pool.wait_ge(h_ps, CH * (g.n - 1))
                nc.gpsimd.tensor_tensor(x2l[g.p][:], flat(x2t[g.p]), x2h[g.p][:].bitcast(F32),
                                        ALU.subtract).then_inc(x2l_sb, 1)

            def query(g):
                pool.wait_ge(x3_sb, EX * GS * (g.n + 1))
                pool.wait_ge(ld_emb[g.p], 16 * GS * (g.turn + 1))
                nc.gpsimd.tensor_tensor(qt[:], x3t[:], emb_in[g.p][:], ALU.add).then_inc(qt_sb, 1)

            def step(gb_, gm, gf):
                if gf is not None and not gf.fresh:
                    load_wsub(gf)
                if gb_ is not None:
                    query(gb_)
                load_emb(gm)
                if gf is not None:
                    split_x2(gf)

            def front(g):
                add_residual()
                pool.wait_ge(ld_tok[1], 16)
                load_wsub(g)
                load_wsub(fixed(1))
                split_x2(g)
                pool.wait_ge(ld_tok[2], 16)

            def back(g):
                for b in (0, 2):
                    pool.wait_ge(x3_sb, tail_mixed(g, b + 1, EX - 1))
                    nc.gpsimd.tensor_tensor(qt[:, b:b + 2, :], x3t[:, b:b + 2, :], x2t[g.p][:, b:b + 2, :],
                                            ALU.add).then_inc(qt_sb, 1)

            pipeline(pool, front, step, back)

        @block.scalar
        def _(act):
            def high_xt(g, samples=ALL):
                act.wait_ge(xt_ps, GS * g.n + samples.stop)
                nc.scalar.activation(flat(xt_h, samples), flat(front_bank(g, samples), samples),
                                     ACT.Identity).then_inc(xth_sb, count(samples))

            def tanh(g, samples=ALL):
                act.wait_ge(z_ps, GS * g.n + samples.stop)
                for t in (th, ths):
                    nc.scalar.activation(flat(t, samples), flat(front_bank(g, samples), samples), ACT.Tanh,
                                         bias=cols[:, 0:1]).then_inc(th_sb, count(samples))

            def subjects():
                for n in range(2):
                    act.wait_ge(subj_ps, n + 1)
                    nc.scalar.copy(subj_t[:, n * GS:(n + 1) * GS, :], hb[n][:]).then_inc(subj_set, 1)

            def exp1(g, samples=ALL):
                act.wait_ge(nmax1_sb, GS * g.n + samples.stop)
                for b in range(samples.start, samples.stop):
                    nc.scalar.activation(p1[:, b, :], front_bank(g, samples)[:, b, :], ACT.Exp, bias=nmax1[:, b:b + 1],
                                         accum_out=sum1[:, b:b + 1]).then_inc(p1_sb, 1)

            def copy_pnt(g, samples=ALL):
                act.wait_ge(pnt_ps, GS * g.n + samples.stop)
                nc.scalar.copy(pnt[:, samples, :], front_bank(g, samples)[:, samples, :]
                               ).then_inc(pnt_sb, count(samples))

            def copy_x1(g, samples=ALL):
                act.wait_ge(x1_ps, GS * g.n + samples.stop)
                nc.scalar.copy(x1t[:, samples, :], front_bank(g, samples)[:, samples, :]
                               ).then_inc(x1_sb, count(samples))

            def split_x2(g):
                act.wait_ge(x2_sb, GS * (g.n + 1))
                if not g.fresh:
                    act.wait_ge(h_ps, CH * (g.n - 1))
                nc.scalar.activation(x2h[g.p][:], flat(x2t[g.p]), ACT.Identity).then_inc(x2h_sb, 1)

            def hidden(g, c):
                act.wait_ge(h_ps, CH * g.n + c + 1)
                if c >= NH or not g.first:
                    act.wait_ge(hid_used, CH * g.n + c + 1 - NH)
                dst = flat(h_sel[c % NH]) if c < FC else h_hi[c % NH][:]
                nc.scalar.activation(dst, flat(hb[c % NH]), ACT.Relu).then_inc(h_sb, 1)

            def expert_out(g, e):
                act.wait_ge(hid_used, CH * g.n + FC * (e + 1))
                if not g.first:
                    act.wait_ge(x3_sb, EX * GS * g.n)
                if e == EX - 1 and isinstance(g.n, int) and g.n == NG - 1:
                    nc.scalar.copy(eo[:, e, :, 0:1], acc_of(g, e)[:, :, 0:1]).then_inc(token0_sb, 1)
                    nc.scalar.copy(eo[:, e, :, 1:], acc_of(g, e)[:, :, 1:]).then_inc(eo_sb, 1)
                else:
                    nc.scalar.copy(eo[:, e].rearrange("p b s -> p (b s)"), flat(acc_of(g, e))).then_inc(eo_sb, 1)

            def gate(g):
                act.wait_ge(gsh_sb, g.n + 1)
                nc.scalar.activation(gexp[:], gsh[:], ACT.Exp).then_inc(gexp_sb, 1)

            def copy_kt(g):
                act.wait_ge(kt_ps, g.n + 1)
                nc.scalar.copy(flat(kt), flat(key_bank(g))).then_inc(kt_sb, 1)

            def copy_x3n(g):
                act.wait_ge(x3n_ps, GS * (g.n + 1))
                nc.scalar.copy(flat(x3n), flat(kb)).then_inc(x3n_sb, 1)

            def exp2(g, samples=ALL):
                act.wait_ge(nmax2_sb, GS * g.n + samples.stop)
                for b in range(samples.start, samples.stop):
                    nc.scalar.activation(p2[:, b, :], back_bank(g, b)[:, b, :], ACT.Exp, bias=nmax2[:, b:b + 1],
                                         accum_out=sum2[:, b:b + 1]).then_inc(p2_sb, 1)

            def copy_p2t(g, samples=ALL):
                act.wait_ge(p2t_ps, GS * g.n + samples.stop)
                nc.scalar.copy(p2t[:, samples, :], back_bank(g, samples.start)[:, samples, :]
                               ).then_inc(p2t_sb, count(samples))

            def front(g):
                h = fixed(1)
                act.wait_ge(pool_set, 5)
                nc.scalar.activation(spare[:], ones[:, 0:1], ACT.Tanh).then_inc(spare_set, 1)
                for half in HALVES:
                    high_xt(g, half)
                act.wait_ge(cols_set, 1)
                for half in HALVES:
                    tanh(g, half)
                subjects()
                for half in HALVES:
                    exp1(g, half)
                high_xt(h)
                act.wait_ge(ld_swi, 16)
                nc.scalar.activation(swi_h[:], swi_in[:], ACT.Identity).then_inc(sw_hi, 1)
                for half in HALVES:
                    copy_pnt(g, half)
                for half in HALVES:
                    copy_x1(g, half)
                act.wait_ge(ld_swo, 16)
                nc.scalar.activation(swo_h[:], swo_in[:], ACT.Identity).then_inc(sw_hi, 1)
                tanh(h)
                split_x2(g)

            def step(gb_, gm, gf):
                gn = None if gf is None or gf.fresh else gf
                for c in range(CH):
                    hidden(gm, c)
                    if c == 0:
                        if gn is not None:
                            high_xt(gn)
                    if c == 1:
                        if gb_ is not None:
                            gate(gb_)
                    if c == 2:
                        if gn is not None:
                            tanh(gn)
                    if c == 3:
                        if gb_ is not None:
                            copy_kt(gb_)
                    if c == 4:
                        if gn is not None:
                            exp1(gn)
                    if c == 6:
                        if gb_ is not None:
                            copy_x3n(gb_)
                    if c == 7:
                        expert_out(gm, 0)
                        if gn is not None:
                            copy_pnt(gn)
                    if c == 8:
                        if gb_ is not None:
                            exp2(gb_)
                        if gn is not None:
                            copy_x1(gn)
                    if c == 10:
                        if gb_ is not None:
                            copy_p2t(gb_)
                        if gn is not None:
                            split_x2(gn)
                    if c == 11:
                        expert_out(gm, 1)
                    if gf is not None and gf.fresh:
                        if c == 1:
                            exp1(gf)
                        if c == 4:
                            copy_pnt(gf)
                        if c == 5:
                            copy_x1(gf)
                        if c == 7:
                            split_x2(gf)
                expert_out(gm, EX - 1)

            def back(g):
                copy_kt(g)
                gate(g)
                act.wait_ge(gw_sb, g.n + 1)
                for b in (2, 3):
                    nc.scalar.activation(x3t[:, b, :], eo[:, 0, b, :], ACT.Identity,
                                         scale=gw[:, b, 0:1]).then_inc(share0_23_sb, 1)
                exp2(g, one(0))
                exp2(g, one(1))
                copy_p2t(g, one(0))
                copy_p2t(g, one(1))
                exp2(g, one(2))
                exp2(g, one(3))
                copy_p2t(g, one(2))
                copy_p2t(g, one(3))

            pipeline(act, front, step, back)

        @block.vector
        def _(dve):
            def constants():
                nc.vector.memset(started[:], 0.0).then_inc(out_rdy, GS)
                nc.vector.memset(rows_rep[:], 0.0).then_inc(rep_zero, 1)
                for q in range(4):
                    nc.vector.memset(is_lo[q * 32:(q + 1) * 32, :], float(q % 2)).then_inc(lo_set, 1)
                dve.wait_ge(pool_set, 5)
                nc.vector.tensor_copy(row[:], row_i[:]).then_inc(tok_set, 1)
                dve.wait_ge(ident_set, 1)
                nc.vector.tensor_copy(identb[:], ident[:]).then_inc(ident_set, 1)

            def repeat_rows():
                dve.wait_ge(ld_rows, 32)
                dve.wait_ge(rep_zero, 1)
                nc.vector.tensor_tensor(rows_rep[:], rows_rep[:],
                                        rows_in[:].rearrange("o n (u a) -> o n u a", u=1)
                                        .to_broadcast([1, 2, GS, A]), ALU.add).then_inc(rows_set, 1)

            def split_w1():
                dve.wait_ge(ld_w1, 16)
                w1_wide = w1_in[:].rearrange("p (o a) -> p o a", o=1).to_broadcast([128, GS, A])
                nc.vector.tensor_copy(w1_h[:], w1_wide).then_inc(w1_set, 1)
                dve.wait_ge(w1_set, 1)
                nc.vector.tensor_tensor(w1_l[:], w1_wide, w1_h[:].bitcast(F32), ALU.subtract).then_inc(w1_set, 1)

            def tokens():
                dve.wait_ge(ld_tokb, 32)
                nc.vector.tensor_copy(tokf[:], tokb[:]).then_inc(tok_set, 1)
                dve.wait_ge(tok_set, 2)
                nc.vector.tensor_scalar(kind[:], tokf[:, 0, :], 2.0, None, ALU.min).then_inc(kind_set, 1)
                nc.vector.tensor_scalar(is0[:], tokf[:, 0, :], 0.0, None, ALU.is_equal).then_inc(cnt_set, 1)
                nc.vector.tensor_scalar(is1[:], tokf[:, 0, :], 1.0, None, ALU.is_equal).then_inc(cnt_set, 1)
                nc.vector.tensor_scalar(onehot[:], tokf[0:NSUB, 1, :], row[0:NSUB, 0:1], None,
                                        ALU.is_equal).then_inc(onehot_set, 1)

            def columns():
                dve.wait_ge(cols_ps, 2)
                dve.wait_ge(lo_set, 4)
                nc.vector.tensor_copy(cols[:], hb[2][:, 2, 0:2]).then_inc(cols_set, 1)
                dve.wait_ge(cols_set, 1)
                nc.vector.tensor_copy(v_h[:], cols[:, 1:2]).then_inc(vs_set, 1)
                dve.wait_ge(vs_set, 1)
                nc.vector.tensor_scalar(v_neg[0:64, :], v_h[0:64, :].bitcast(F32), -1.0, None,
                                        ALU.mult).then_inc(vs_set, 1)
                nc.vector.tensor_tensor(v_neg[64:128, :], v_h[64:128, :].bitcast(F32), cols[64:128, 1:2],
                                        ALU.subtract).then_inc(vs_set, 1)
                dve.wait_ge(vs_set, 3)
                nc.vector.tensor_scalar(vs[:], ones[:], v_neg[:, 0:1], None, ALU.mult).then_inc(vs_set, 1)

            def make_masks(g):
                if g.first:
                    dve.wait_ge(kind_set, 1)
                    dve.wait_ge(sides_set, 2)
                else:
                    dve.wait_ge(sc_ps, GS * g.n)
                for b in range(GS):
                    nc.vector.tensor_scalar(mask[:, b, :], side_of[:], kind[:, bass.ds(g.n * GS + b, 1)], NEG,
                                            ALU.is_equal, ALU.mult).then_inc(mask_sb, 1)

            def counts():
                nc.vector.tensor_scalar(up[:], row[:], 1.0, float(2 - S), ALU.mult, ALU.add).then_inc(cnt_set, 1)
                nc.vector.tensor_scalar(down[:], row[:], -1.0, 1.0, ALU.mult, ALU.add).then_inc(cnt_set, 1)
                dve.wait_ge(cnt_set, 4)
                nc.vector.tensor_scalar(cnt[:], is0[:], up[:, 0:1], float(S - 1), ALU.mult, ALU.add).then_inc(cnt_set, 1)
                dve.wait_ge(cnt_set, 5)
                nc.vector.scalar_tensor_tensor(out=cnt[:], in0=is1[:], scalar=down[:, 0:1], in1=cnt[:],
                                               op0=ALU.mult, op1=ALU.add).then_inc(cnt_set, 1)

            def add_residual():
                dve.wait_ge(ld_subj, 16)
                nc.vector.tensor_tensor(subj_in[:, 0:GS, :], subj_in[:, 0:GS, :], ident_wide,
                                        ALU.add).then_inc(subj_in_set, 1)

            def copy_bias():
                dve.wait_ge(bias_ps, 1)
                nc.vector.tensor_copy(bias[:], hb[2][:, 0, 0:B]).then_inc(bias_set, 1)

            def low_xt(g, samples=ALL):
                dve.wait_ge(xth_sb, GS * g.n + samples.stop)
                nc.vector.tensor_tensor(flat(xt_l, samples), flat(front_bank(g, samples), samples),
                                        flat(xt_h, samples).bitcast(F32), ALU.subtract).then_inc(xtl_sb, count(samples))

            def stack_tanh(g, samples=ALL):
                dve.wait_ge(th_sb, 2 * (GS * g.n + samples.stop))
                nc.vector.scalar_tensor_tensor(out=flat(ths, samples), in0=flat(ths, samples).bitcast(F32),
                                               scalar=is_lo[:, 0:1], in1=flat(th, samples),
                                               op0=ALU.mult, op1=ALU.subtract).then_inc(ths_sb, count(samples))

            def max1(g, samples=ALL):
                dve.wait_ge(sc_ps, GS * g.n + samples.stop)
                nc.vector.tensor_reduce(nmax1[:, samples], front_bank(g, samples)[:, samples, :], AX, ALU.max,
                                        negate=True).then_inc(nmax1_sb, count(samples))

            def norm1(g, samples=ALL):
                dve.wait_ge(p1_sb, GS * g.n + samples.stop)
                if g.first:
                    dve.wait_ge(cnt_set, 6)
                nc.vector.tensor_tensor(den1[:, samples], sum1[:, samples],
                                        cnt[:, bass.ds(g.n * GS + samples.start, count(samples))],
                                        ALU.mult).then_inc(den1_sb, count(samples))
                dve.wait_ge(den1_sb, GS * g.n + samples.stop)
                nc.vector.reciprocal(rec1[:, samples], den1[:, samples]).then_inc(rec1_sb, count(samples))
                dve.wait_ge(rec1_sb, GS * g.n + samples.stop)
                for b in range(samples.start, samples.stop):
                    nc.vector.scalar_tensor_tensor(out=pn[:, b, :], in0=p1[:, b, :], scalar=rec1[:, b:b + 1],
                                                   in1=ident[:], op0=ALU.mult, op1=ALU.add).then_inc(pn_sb, 1)

            def add_bias(g, samples=ALL):
                dve.wait_ge(x2_ps, GS * g.n + samples.stop)
                if not g.fresh:
                    dve.wait_ge(x3_sb, EX * GS * (g.n - 1))
                nc.vector.tensor_tensor(x2t[g.p][:, samples, :], front_bank(g, samples)[:, samples, :],
                                        bias[:, bass.ds(g.n * GS + samples.start, count(samples))]
                                        .rearrange("p (b o) -> p b o", o=1).to_broadcast([128, count(samples), S]),
                                        ALU.add).then_inc(x2_sb, count(samples))

            def hidden_low(g, c):
                dve.wait_ge(h_sb, CH * g.n + c + 1)
                nc.vector.scalar_tensor_tensor(out=h_lo[c % NH][:], in0=flat(hb[c % NH]), scalar=0.0,
                                               in1=h_hi[c % NH][:].bitcast(F32), op0=ALU.max,
                                               op1=ALU.subtract).then_inc(hl_sb, 1)

            def gate1(g):
                dve.wait_ge(g1_ps, g.n + 1)
                nc.vector.scalar_tensor_tensor(
                    out=gprod[:], in0=kb[:, 0, 0:GS].rearrange("p (b o) -> p b o", o=1).to_broadcast([128, GS, EX]),
                    scalar=0.0, in1=g2_sb[:].rearrange("p (o e) -> p o e", o=1).to_broadcast([128, GS, EX]),
                    op0=ALU.max, op1=ALU.mult).then_inc(gprod_sb, 1)

            def gate2(g):
                dve.wait_ge(g2_ps, g.n + 1)
                logits = kb[:, 1, 0:GS * EX].rearrange("p (b e) -> p b e", e=EX)
                nc.vector.tensor_reduce(gnmax[:], logits, AX, ALU.max, negate=True).then_inc(gnmax_sb, 1)
                dve.wait_ge(gnmax_sb, g.n + 1)
                nc.vector.tensor_tensor(gsh[:], logits, gnmax[:].rearrange("p (b o) -> p b o", o=1)
                                        .to_broadcast([128, GS, EX]), ALU.add).then_inc(gsh_sb, 1)

            def gate3(g):
                dve.wait_ge(gexp_sb, g.n + 1)
                nc.vector.tensor_reduce(gsum[:], gexp[:], AX, ALU.add).then_inc(gsum_sb, 1)
                dve.wait_ge(gsum_sb, g.n + 1)
                nc.vector.reciprocal(grec[:], gsum[:]).then_inc(grec_sb, 1)
                dve.wait_ge(grec_sb, g.n + 1)
                nc.vector.tensor_tensor(gw[:], gexp[:], grec[:].rearrange("p (b o) -> p b o", o=1)
                                        .to_broadcast([128, GS, EX]), ALU.mult).then_inc(gw_sb, 1)
                dve.wait_ge(gw_sb, g.n + 1)

            def shares(g, e):
                for b in range(GS):
                    if e:
                        dve.wait_ge(x3_sb, EX * GS * g.n + GS * (e - 1) + b + 1)
                    add_share(g, b, e, x3t if e else x2t[g.p])

            def add_share(g, b, e, to):
                nc.vector.scalar_tensor_tensor(out=x3t[:, b, :], in0=eo[:, e, b, :], scalar=gw[:, b, e:e + 1],
                                               in1=to[:, b, :], op0=ALU.mult, op1=ALU.add).then_inc(x3_sb, 1)

            def max2(g, samples=ALL):
                dve.wait_ge(at_ps, GS * g.n + samples.stop)
                nc.vector.tensor_reduce(nmax2[:, samples], back_bank(g, samples.start)[:, samples, :], AX, ALU.max,
                                        negate=True).then_inc(nmax2_sb, count(samples))

            def norm2(g, samples=ALL):
                dve.wait_ge(p2_sb, GS * g.n + samples.stop)
                nc.vector.reciprocal(rec2[:, samples], sum2[:, samples]).then_inc(rec2_sb, count(samples))

            def result(g, samples=ALL):
                dve.wait_ge(pv_ps, GS * g.n + samples.stop)
                dve.wait_ge(x3n_sb, g.n + 1)
                dve.wait_ge(rec2_sb, GS * g.n + samples.stop)
                for b in range(samples.start, samples.stop):
                    nc.vector.scalar_tensor_tensor(out=out_sb[:, bass.ds(g.n * GS + b, 1), :],
                                                   in0=back_bank(g, b)[:, b, :], scalar=rec2[:, b:b + 1],
                                                   in1=x3n[:, b, :], op0=ALU.mult, op1=ALU.add).then_inc(out_rdy, 1)

            def front(g):
                h = fixed(1)
                constants()
                repeat_rows()
                split_w1()
                for half in HALVES:
                    low_xt(g, half)
                columns()
                tokens()
                add_residual()
                make_masks(g)
                for half in HALVES:
                    stack_tanh(g, half)
                for half in HALVES:
                    max1(g, half)
                counts()
                copy_bias()
                for half in HALVES:
                    norm1(g, half)
                low_xt(h)
                dve.wait_ge(sw_hi, 1)
                nc.vector.tensor_tensor(swi_l[:], swi_in[:], swi_h[:].bitcast(F32), ALU.subtract).then_inc(sw_lo, 1)
                make_masks(h)
                for half in HALVES:
                    add_bias(g, half)
                dve.wait_ge(sw_hi, 2)
                nc.vector.tensor_tensor(swo_l[:], swo_in[:], swo_h[:].bitcast(F32), ALU.subtract).then_inc(sw_lo, 1)
                stack_tanh(h)

            def step(gb_, gm, gf):
                gn = None if gf is None or gf.fresh else gf
                for c in range(CH):
                    if c >= FC:
                        hidden_low(gm, c)
                    if c == 0:
                        if gb_ is not None:
                            gate1(gb_)
                        if gn is not None:
                            make_masks(gn)
                    if c == 1:
                        if gb_ is not None:
                            gate2(gb_)
                        if gn is not None:
                            low_xt(gn)
                        if gb_ is not None:
                            gate3(gb_)
                            shares(gb_, 0)
                            shares(gb_, 1)
                        if gn is not None:
                            stack_tanh(gn)
                    if c == 3:
                        if gb_ is not None:
                            shares(gb_, 2)
                        if gn is not None:
                            max1(gn)
                    if c == 6:
                        if gn is not None:
                            norm1(gn)
                    if c == 7:
                        if gb_ is not None:
                            max2(gb_)
                    if c == 9:
                        if gn is not None:
                            add_bias(gn)
                        if gb_ is not None:
                            norm2(gb_)
                    if gf is not None and gf.fresh:
                        if c == 1:
                            max1(gf)
                            norm1(gf)
                        if c == 5:
                            add_bias(gf)
                if gb_ is not None:
                    result(gb_)

            def back(g):
                def pair_shares(b, e):
                    for i in (b, b + 1):
                        if e == 1:
                            dve.wait_ge(*((share0_01_sb, i + 1) if b == 0 else (share0_23_sb, i - 1)))
                            dve.wait_ge(eo_sb, EX * (g.n + 1))
                        else:
                            dve.wait_ge(x3_sb, tail_mixed(g, i, e - 1))
                        add_share(g, i, e, x3t)

                gate1(g)
                gate2(g)
                gate3(g)
                for b in (0, 1):
                    nc.vector.tensor_scalar(x3t[:, b, :], eo[:, 0, b, :], gw[:, b, 0:1], None,
                                            ALU.mult).then_inc(share0_01_sb, 1)
                pair_shares(0, 1)
                pair_shares(0, 2)
                pair_shares(2, 1)
                max2(g, one(0))
                max2(g, one(1))
                pair_shares(2, 2)
                norm2(g, one(0))
                norm2(g, one(1))
                max2(g, one(2))
                max2(g, one(3))
                norm2(g, one(2))
                norm2(g, one(3))
                dve.wait_ge(x3n_ps, GS * (g.n + 1))
                nc.vector.tensor_copy(x3n[:], kb[:]).then_inc(x3n_sb, 1)
                result(g, one(0))
                result(g, one(1))
                result(g, one(2))
                result(g, one(3))

            pipeline(dve, front, step, back)

        @block.tensor
        def _(pe):
            def warm(n):
                for _ in range(n):
                    nc.tensor.matmul(flat(ab[0]), zeros[:, 0:128], zeros[:], start=True, stop=True)

            def columns():
                pe.wait_ge(rows_set, 1)
                pe.wait_ge(pool_set, 5)
                for n in range(2):
                    nc.tensor.matmul(hb[2][:, 2, n:n + 1], rows_rep[:, n].rearrange("o b a -> o (b a)"), ones[0:1, 0:1],
                                     start=True, stop=True).then_inc(cols_ps, 1)

            def subjects():
                for n in range(NSUB):
                    if n % GS == 0:
                        pe.wait_ge((subj_in_set, subj_in2_set)[n // GS], 1)
                    t = nc.tensor.transpose(hb[n // GS][:, n % GS, :], subj_in[:, n, :], ident[:])
                    if n % GS == GS - 1:
                        t.then_inc(subj_ps, 1)

            def biases():
                pe.wait_ge(onehot_set, 1)
                pe.wait_ge(ld_bias, 16)
                pe.wait_ge(cols_set, 1)
                nc.tensor.matmul(hb[2][:, 0, 0:B], bias_rows[:], onehot[:], start=True, stop=True).then_inc(bias_ps, 1)

            def x_turn(g, samples=ALL):
                pe.wait_ge(ld_x[g.p], 16 * (g.turn + 1))
                if not g.fresh:
                    pe.wait_ge(x2_sb, GS * g.n)
                for b in range(samples.start, samples.stop):
                    t = nc.tensor.transpose(front_bank(g, samples)[:, b, :], x_in[g.p][:, b, :], ident[:])
                t.then_inc(xt_ps, count(samples))

            def z(g, samples=ALL):
                pe.wait_ge(xtl_sb, GS * g.n + samples.stop)
                bank, high, low = flat(front_bank(g, samples), samples), flat(xt_h, samples), flat(xt_l, samples)
                nc.tensor.matmul(bank, flat(w1_h), high, start=True, stop=False)
                nc.tensor.matmul(bank, flat(w1_l), high, start=False, stop=False)
                nc.tensor.matmul(bank, flat(w1_h), low, start=False, stop=True).then_inc(z_ps, count(samples))

            def scores1(g, samples=ALL):
                pe.wait_ge(ths_sb, GS * g.n + samples.stop)
                pe.wait_ge(mask_sb, GS * g.n + samples.stop)
                bank = flat(front_bank(g, samples), samples)
                nc.tensor.matmul(bank, identb[:], flat(mask, samples), start=True, stop=False)
                nc.tensor.matmul(bank, vs[:], flat(ths, samples), start=False, stop=True).then_inc(sc_ps, count(samples))

            def pn_turn(g, samples=ALL):
                pe.wait_ge(pn_sb, GS * g.n + samples.stop)
                for b in range(samples.start, samples.stop):
                    t = nc.tensor.transpose(front_bank(g, samples)[:, b, :], pn[:, b, :], ident[:])
                t.then_inc(pnt_ps, count(samples))

            def pooled(g, samples=ALL):
                pe.wait_ge(pnt_sb, GS * g.n + samples.stop)
                for b in range(samples.start, samples.stop):
                    m = nc.tensor.matmul(front_bank(g, samples)[:, b, :], x_in[g.p][:, b, :], pnt[:, b, :],
                                         start=True, stop=True)
                m.then_inc(x1_ps, count(samples))

            def subject(g, samples=ALL):
                pe.wait_ge(x1_sb, GS * g.n + samples.stop)
                if g.first:
                    if samples.start == 0:
                        pe.wait_ge(ld_wsub0[0], 16 * GS // 2)
                    else:
                        pe.wait_ge(ld_wsub0[1], 16 * (GS // 2 - 1))
                        pe.wait_ge(ld_wsub_last, 16)
                else:
                    pe.wait_ge(ld_wsub[g.p], 16 * GS * (g.turn + g.p))
                for b in range(samples.start, samples.stop):
                    m = nc.tensor.matmul(front_bank(g, samples)[:, b, :], wsub[g.p][:, b, :], x1t[:, b, :],
                                         start=True, stop=True)
                m.then_inc(x2_ps, count(samples))

            def hid(g, c):
                e, k = c // FC, c % FC
                cols = slice(k * 128, (k + 1) * 128)
                dst = hb[c % NH]
                if c >= NH or not g.first:
                    pe.wait_ge(h_sb, CH * g.n + c + 1 - NH)
                    if c >= NH + FC:
                        pe.wait_ge(hl_sb, (CH - FC) * g.n + c + 1 - NH - FC)
                    elif c < NH:
                        pe.wait_ge(hl_sb, (CH - FC) * g.n + c + 1 - NH)
                if e == 0:
                    if k == 0:
                        pe.wait_ge(ld_wi[g.p], 16 * GS * (g.turn + 1))
                    for b in range(GS):
                        if k == 0 and (b == 0 or g.first and b == GS // 2):
                            pe.wait_ge(x2_sb, GS * g.n + (GS // 2 + b if g.first else GS))
                        m = nc.tensor.matmul(dst[:, b, :], wi_in[g.p][:, b, cols], x2t[g.p][:, b, :],
                                             start=True, stop=True)
                else:
                    if e == 1 and k == 0:
                        pe.wait_ge(x2l_sb, g.n + 1)
                        if g.first:
                            pe.wait_ge(sw_lo, 1)
                    nc.tensor.matmul(flat(dst), swi_h[:, e - 1, cols], x2h[g.p][:], start=True, stop=False)
                    nc.tensor.matmul(flat(dst), swi_h[:, e - 1, cols], x2l[g.p][:], start=False, stop=False)
                    m = nc.tensor.matmul(flat(dst), swi_l[:, e - 1, cols], x2h[g.p][:], start=False, stop=True)
                m.then_inc(h_ps, 1)

            def outp(g, c):
                e, k = c // FC, c % FC
                acc = acc_of(g, e)
                if k == 0 and (e >= 2 or not g.first):
                    pe.wait_ge(eo_sb, EX * g.n + e - 1)
                if e == 0:
                    pe.wait_ge(h_sb, CH * g.n + c + 1)
                    if k == 0:
                        pe.wait_ge(ld_wo[g.p], 16 * GS * (g.turn + 1))
                    for b in range(GS):
                        m = nc.tensor.matmul(acc[:, b, :], wo_in[g.p][:, b, k, :], h_sel[c % NH][:, b, :],
                                             start=k == 0 and b == 0, stop=k == FC - 1, skip_group_check=True)
                else:
                    if e == 1 and k == 0 and g.first:
                        pe.wait_ge(sw_lo, 2)
                    pe.wait_ge(hl_sb, (CH - FC) * g.n + c + 1 - FC)
                    hh, hl = h_hi[c % NH][:], h_lo[c % NH][:]
                    nc.tensor.matmul(flat(acc), swo_h[:, e - 1, k, :], hh, start=k == 0, stop=False)
                    nc.tensor.matmul(flat(acc), swo_l[:, e - 1, k, :], hh, start=False, stop=False)
                    m = nc.tensor.matmul(flat(acc), swo_h[:, e - 1, k, :], hl, start=False, stop=k == FC - 1)
                m.then_inc(hid_used, 1)

            def gate1(g):
                pe.wait_ge(out_rdy, GS * (g.n + 1))
                for e in range(EX):
                    if e == EX - 1 and isinstance(g.n, int) and g.n == NG - 1:
                        pe.wait_ge(token0_sb, 1)
                    else:
                        pe.wait_ge(eo_sb, EX * g.n + e + 1)
                    m = nc.tensor.matmul(kb[:, 0, 0:GS], g1_sb[:, e, :], eo[:, e, :, 0], start=e == 0, stop=e == EX - 1)
                m.then_inc(g1_ps, 1)

            def gate2(g):
                pe.wait_ge(gprod_sb, g.n + 1)
                nc.tensor.matmul(kb[:, 1, 0:GS * EX], ones[:], gprod[:].rearrange("p b e -> p (b e)"),
                                 start=True, stop=True).then_inc(g2_ps, 1)

            def key_turn(g):
                if key_bank(g) is kb:
                    pe.wait_ge(gsh_sb, g.n + 1)
                pe.wait_ge(ld_side[g.p], 16 * (g.turn + 1))
                for b in range(GS):
                    t = nc.tensor.transpose(key_bank(g)[:, b, :], side_in[g.p][:, b, :], ident[:])
                t.then_inc(kt_ps, 1)

            def x3_turn(g):
                pe.wait_ge(x3_sb, EX * GS * (g.n + 1))
                pe.wait_ge(kt_sb, g.n + 1)
                for b in range(GS):
                    t = nc.tensor.transpose(kb[:, b, :], x3t[:, b, :], ident[:])
                t.then_inc(x3n_ps, GS)

            def scores2(g):
                pe.wait_ge(qt_sb, g.n + 1)
                pe.wait_ge(x3n_sb, g.n + 1)
                for b in range(GS):
                    m = nc.tensor.matmul(kb[:, b, :], qt[:, b, :], kt[:, b, :], start=True, stop=True)
                m.then_inc(at_ps, GS)

            def p2_turn(g, samples=ALL):
                pe.wait_ge(p2_sb, GS * g.n + samples.stop)
                for b in range(samples.start, samples.stop):
                    t = nc.tensor.transpose(back_bank(g, b)[:, b, :], p2[:, b, :], ident[:])
                t.then_inc(p2t_ps, count(samples))

            def attend(g, samples=ALL):
                pe.wait_ge(p2t_sb, GS * g.n + samples.stop)
                for b in range(samples.start, samples.stop):
                    m = nc.tensor.matmul(back_bank(g, b)[:, b, :], p2t[:, b, :], side_in[g.p][:, b, :],
                                         start=True, stop=True)
                m.then_inc(pv_ps, count(samples))

            def front(g):
                h = fixed(1)
                pe.wait_ge(pool_set, 2)
                warm(5)
                pe.wait_ge(ident_set, 1)
                for half in HALVES:
                    x_turn(g, half)
                columns()
                warm(1)
                pe.wait_ge(w1_set, 2)
                for half in HALVES:
                    z(g, half)
                subjects()
                pe.wait_ge(vs_set, 4)
                pe.wait_ge(ident_set, 2)
                for half in HALVES:
                    scores1(g, half)
                biases()
                x_turn(h)
                warm(5)
                pn_turn(g, HALVES[0])
                warm(3)
                pn_turn(g, HALVES[1])
                for half in HALVES:
                    pooled(g, half)
                pe.wait_ge(bias_set, 1)
                subject(g, HALVES[0])
                z(h)
                subject(g, HALVES[1])
                pe.wait_ge(subj_set, 2)

            def step(gb_, gm, gf):
                gn = None if gf is None or gf.fresh else gf
                for c in range(CH + LAG):
                    if c < CH:
                        hid(gm, c)
                    if c == 0:
                        if gb_ is not None:
                            gate1(gb_)
                        if gn is not None:
                            x_turn(gn)
                    if c == 1:
                        if gb_ is not None:
                            gate2(gb_)
                    if c == 3:
                        if gn is not None:
                            z(gn)
                    if c == 7:
                        if gb_ is not None:
                            scores2(gb_)
                    if c == 8:
                        if gn is not None:
                            pn_turn(gn)
                    if c == 11:
                        if gb_ is not None:
                            attend(gb_)
                    if c >= LAG:
                        outp(gm, c - LAG)
                    if c == 4:
                        if gb_ is not None:
                            key_turn(gb_)
                        if gn is not None:
                            scores1(gn)
                    if c == 5:
                        if gb_ is not None:
                            x3_turn(gb_)
                    if c == 9:
                        if gn is not None:
                            pooled(gn)
                    if c == 10:
                        if gb_ is not None:
                            p2_turn(gb_)
                        if gn is not None:
                            subject(gn)
                    if gf is not None and gf.fresh:
                        if c == 1:
                            scores1(gf)
                        if c == 4:
                            pn_turn(gf)
                        if c == 5:
                            pooled(gf)
                        if c == 6:
                            subject(gf)
                        if c == CH:
                            pe.wait_ge(ld_gate, 32)

            def back(g):
                gate1(g)
                key_turn(g)
                gate2(g)
                pe.wait_ge(ld_emb[g.p], 16 * GS * (g.turn + 1))
                pe.wait_ge(kt_sb, g.n + 1)
                for b in range(GS):
                    scores = back_bank(g, b)[:, b, :]
                    nc.tensor.matmul(scores, emb_in[g.p][:, b, :], kt[:, b, :], start=True, stop=False)
                    nc.tensor.matmul(scores, x2t[g.p][:, b, :], kt[:, b, :], start=False, stop=False)

                def scores_of_mix(b):
                    pe.wait_ge(x3_sb, tail_mixed(g, b, EX - 1))
                    nc.tensor.matmul(back_bank(g, b)[:, b, :], x3t[:, b, :], kt[:, b, :],
                                     start=False, stop=True).then_inc(at_ps, 1)

                scores_of_mix(0)
                scores_of_mix(1)
                p2_turn(g, one(0))
                scores_of_mix(2)
                scores_of_mix(3)
                p2_turn(g, one(1))
                attend(g, one(0))
                pe.wait_ge(qt_sb, g.n + 2)
                pe.wait_ge(gsh_sb, g.n + 1)
                for b in range(GS):
                    t = nc.tensor.transpose(kb[:, b, :], qt[:, b, :], ident[:])
                t.then_inc(x3n_ps, GS)
                p2_turn(g, one(2))
                attend(g, one(1))
                p2_turn(g, one(3))
                for b in (2, 3):
                    attend(g, one(b))

            pipeline(pe, front, step, back)


_INS = ["x", "itok_B_0_2", "itok_B_0_7", "fside_BxSxS_0", "itok_B_0_5", "L0_cond_W1", "L0_cond_b1", "L0_cond_v",
        "L1_cond_weight", "L1_cond_bias", "L2_cond_wi", "L2_cond_wo", "L2_cond_swi", "L2_cond_swo", "L2_cond_g1",
        "L2_cond_g2", "L3_cond_braak_embed"]


def kernel(**inputs):
    import concourse.bacc as bacc
    import numpy as np
    from concourse.bass_utils import run_bass_kernel_spmd

    nc = bacc.Bacc("TRN2", target_bir_lowering=False, num_devices=1)
    arrays, args = {}, []
    for name in _INS:
        a = np.ascontiguousarray(inputs[name])
        arrays[f"in_{name}"] = a
        args.append(nc.dram_tensor(f"in_{name}", a.shape, mybir.dt.from_np(a.dtype), kind="ExternalInput").ap())
    out = nc.dram_tensor("out", inputs["x"].shape, F32, kind="ExternalOutput").ap()
    build(nc, *args, out)
    return run_bass_kernel_spmd(nc, [arrays], core_ids=[0]).results[0]["out"]
```
